# Optimizing a Trainium2 kernel written in Bass

```python
import numpy as np
import jax
import jax.numpy as jnp

def _softmax(x, axis=-1):
    return jax.nn.softmax(x, axis=axis)

def _gelu(x):
    return jax.nn.gelu(x, approximate=True)

def _silu(x):
    return jax.nn.silu(x)

def _sigmoid(x):
    return jax.nn.sigmoid(x)

def _layernorm(x, axis=-1, eps=1e-05):
    m = jnp.mean(x, axis=axis, keepdims=True)
    v = jnp.var(x, axis=axis, keepdims=True)
    return (x - m) / jnp.sqrt(v + eps)

def _scatter_add(tgt, idx, src, axis=0):
    return tgt.at[idx].add(src)

def _segment_sum(src, seg, n):
    return jax.ops.segment_sum(src, seg, n)
kernel_name = 'mk_recurrent_d1_jaxref_r8_7f5f96'

def setup_inputs(seed: int=0):
    np.random.seed(seed)
    _w = jnp.asarray

    def _L0_attn_setup():
        import jax, jax.numpy as jnp
        import numpy as np
        B, L, DM, H, N = (4, 512, 256, 32, 128)
        HD = DM // H
        key = jax.random.key(seed)
        ks = jax.random.split(key, 6)
        x = jax.random.normal(ks[0], (B, L, DM), dtype=jnp.float32)
        Wx = jax.random.normal(ks[1], (DM, 2 * N + H), dtype=jnp.float32) * 0.02
        Wg = jax.random.normal(ks[2], (DM, DM), dtype=jnp.float32) * 0.02
        bg = jnp.zeros((DM,), dtype=jnp.float32)
        Wo = jax.random.normal(ks[3], (DM, DM), dtype=jnp.float32) * 0.02
        A = -1.0 + 0.1 * jax.random.normal(ks[4], (H, N), dtype=jnp.float32)
        Dp = jnp.ones((H,), dtype=jnp.float32)
        return {'x': x, 'Wx': Wx, 'Wg': Wg, 'bg': bg, 'Wo': Wo, 'A': A, 'Dp': Dp}
    _L0_attn_in = _L0_attn_setup()

    def _L0_ffn_setup():
        import jax, jax.numpy as jnp
        import numpy as np
        B, S, D_IN, D_OUT = (4, 256, 256, 256)
        EPS = 1e-10
        key = jax.random.key(seed)
        kx, kw, kb = jax.random.split(key, 3)
        x = jax.random.normal(kx, (B, S, D_IN), dtype=jnp.float32)
        weight = jax.random.normal(kw, (D_OUT, D_IN), dtype=jnp.float32) * 0.02
        bias = jax.random.normal(kb, (D_OUT,), dtype=jnp.float32) * 0.02
        return {'x': x, 'weight': weight, 'bias': bias}
    _L0_ffn_in = _L0_ffn_setup()
    _d = {'L0_attn_x': _L0_attn_in['x'], 'L0_attn_Wx': _L0_attn_in['Wx'], 'L0_attn_Wg': _L0_attn_in['Wg'], 'L0_attn_bg': _L0_attn_in['bg'], 'L0_attn_Wo': _L0_attn_in['Wo'], 'L0_attn_A': _L0_attn_in['A'], 'L0_attn_Dp': _L0_attn_in['Dp'], 'L0_ffn_weight': _L0_ffn_in['weight'], 'L0_ffn_bias': _L0_ffn_in['bias']}
    _x0 = _d['L0_attn_x']
    _d['L0_attn_x'] = jax.random.normal(jax.random.fold_in(jax.random.key(seed), 1), (2, 2048, 256), dtype=_x0.dtype)
    del _x0
    return _d

def reference(L0_attn_x, L0_attn_Wx, L0_attn_Wg, L0_attn_bg, L0_attn_Wo, L0_attn_A, L0_attn_Dp, L0_ffn_weight, L0_ffn_bias):

    def _L0_attn_ref(x, Wx, Wg, bg, Wo, A, Dp):
        import jax, jax.numpy as jnp
        import numpy as np
        B, L, DM, H, N = (4, 512, 256, 32, 128)
        HD = DM // H
        b, l, dm = x.shape
        h, n = A.shape
        hd = dm // h
        ssm_params = x @ Wx
        B_ssm = ssm_params[..., :n]
        C_ssm = ssm_params[..., n:2 * n]
        delta_bias = ssm_params[..., 2 * n:]
        gate = jax.nn.sigmoid(x @ Wg + bg)
        delta = jax.nn.softplus(delta_bias[..., :, None] + B_ssm[..., None, :])
        d_seq = jnp.moveaxis(delta, 1, 0)
        h0 = jnp.zeros((b, h, n), dtype=x.dtype)

        def step(hst, d_t):
            hst = jnp.exp(d_t * A) * hst + d_t * d_t
            return (hst, hst)
        _, hs = jax.lax.scan(step, h0, d_seq)
        hs = jnp.moveaxis(hs, 0, 1)
        y = jnp.einsum('blhn,bln->blh', hs, C_ssm)
        xg = x.reshape(b, l, h, hd)
        yh = y[..., None] + xg * Dp[None, None, :, None]
        y_full = yh.reshape(b, l, dm) * gate
        return y_full @ Wo

    def _L0_ffn_ref(x, weight, bias):
        import jax, jax.numpy as jnp
        import numpy as np
        B, S, D_IN, D_OUT = (4, 256, 256, 256)
        EPS = 1e-10
        scale = jnp.mean(jnp.abs(weight))
        w_t = jnp.clip(jnp.round(weight / (scale + EPS)), -1.0, 1.0)
        w_ste = weight + jax.lax.stop_gradient(w_t * scale - weight)
        return jnp.einsum('bsi,oi->bso', x, w_ste) + bias
    x = L0_attn_x
    xn = _layernorm(x, axis=-1)
    s = _L0_attn_ref(xn, L0_attn_Wx, L0_attn_Wg, L0_attn_bg, L0_attn_Wo, L0_attn_A, L0_attn_Dp)
    g = _silu(_L0_ffn_ref(xn, L0_ffn_weight, L0_ffn_bias))
    x = x + s * g
    return x

_drawn_inputs = setup_inputs


def setup_inputs(seed=0):
    import zlib

    import numpy as np

    out = dict(_drawn_inputs(seed))
    spreads = {'L0_attn_bg': (0.0, 2.0), 'L0_attn_Dp': (1.0, 0.6)}
    factors = {'L0_attn_Wg': 4.275, 'L0_attn_A': 200.0, 'L0_ffn_bias': 7.047}
    for name, (base, spread) in spreads.items():
        noise = np.random.default_rng([zlib.crc32(name.encode()), seed]).standard_normal(out[name].shape)
        drawn = base * np.exp(spread * noise) if base else spread * noise
        out[name] = jnp.asarray(drawn.astype(out[name].dtype))
    for name, factor in factors.items():
        out[name] = (out[name] * factor).astype(out[name].dtype)
    return out
```

```python
from contextlib import ExitStack

import concourse.bass as bass
import numpy as np
from concourse import mybir

F32 = mybir.dt.float32
BF16 = mybir.dt.bfloat16
ALU = mybir.AluOpType
ACT = mybir.ActivationFunctionType
AX_X = mybir.AxisListType.X

P = 128
BLK = 32
STEP = 256
SP_CLAMP = 40.0
LN_EPS = 1e-5
W_EPS = 1e-10

C_ID, C_MASK, C_EYE, C_KEEP, C_REP = 0, 128, 160, 192, 194
C_COLS = C_REP + 256


def shape_constants(heads, dm):
    t = np.zeros((P, C_COLS), np.float32)
    row = np.arange(P)
    t[:, C_ID:C_ID + P] = np.eye(P)
    t[:, C_MASK:C_MASK + BLK] = row[:, None] % BLK == np.arange(BLK)
    t[:, C_EYE:C_EYE + heads] = (row[:, None] % heads == np.arange(heads)) & (row[:, None] < 3 * heads)
    t[:, C_KEEP] = np.where(row >= heads, -1.0, 0.0)
    t[:, C_KEEP + 1] = np.where(row >= 2 * heads, -1.0, 0.0)
    t[:heads, C_REP:C_REP + dm] = np.arange(dm) // (dm // heads) == np.arange(heads)[:, None]
    return t


def program(nc, x, Wx, Wg, bg, Wo, A, Dp, Wf, bf, consts, out):
    batch, length, DM = x.shape
    H, N = A.shape
    assert N == P and DM == 2 * P and H == 32 and Wx.shape[1] == 2 * N + H
    TOK = batch * length
    SEG = 1024
    SEGS = TOK // SEG
    SEGS_PER_ROW = length // SEG
    assert SEGS == 4 and SEGS_PER_ROW == 2
    HG = 8
    GROUPS = H // HG
    STEPS = SEG // STEP
    assert STEPS == GROUPS == 4
    TT = STEP // P
    TILES = SEG // P
    PARTS = 4
    NSTEPS = SEGS * STEPS
    K3 = 3 * H

    with ExitStack() as ctx:
        def sb(name, shape, dt=F32):
            return ctx.enter_context(nc.sbuf_tensor(name, shape, dt))

        def ps(name, shape):
            return ctx.enter_context(nc.psum_tensor(name, shape, F32))

        def sem(name):
            return ctx.enter_context(nc.semaphore(name))

        z_ps = ps("z_ps", [P, 2, SEG])
        y_ps = ps("y_ps", [P, 512])
        m0 = ps("m0", [P, 512])
        m12 = ps("m12", [P, 2, 512])

        cst = sb("cst", [P, C_COLS])
        ident = cst[:, C_ID:C_ID + P]
        mask = cst[:, C_MASK:C_MASK + BLK]
        ident_bf = sb("ident_bf", [P, P], BF16)
        sel = sb("sel", [P, H, P], BF16)
        wx = sb("wx", [P, 2, 2 * N + H])
        wdb = sb("wdb", [P, 2, 3, H])
        wgn = sb("wgn", [P, 2, DM])
        wo = sb("wo", [P, 2, DM])
        wfn = sb("wfn", [P, 2, DM])
        rows = sb("rows", [1, 2, DM])
        ones = sb("ones", [P, STEP])
        dp_in = sb("dp_in", [H, 1])
        dp = sb("dp", [P, 2])
        a_in = sb("a_in", [H, P])
        a_t = sb("a_t", [P, H])
        half = sb("half", [P, TT])
        eps = sb("eps", [P, TT])
        wstat = sb("wstat", [P, 8])

        e_sb = sb("e_sb", [P, 2, SEG])
        d_sb = sb("d_sb", [P, 2, SEG])
        a_sb = sb("a_sb", [P, 2, SEG])
        b_sb = sb("b_sb", [P, 2, SEG])
        hs = sb("hs", [P, 2, HG, SEG])
        carry = sb("carry", [P, H])
        bsp = sb("bsp", [P, 2, 3, SEG], BF16)
        dsp = sb("dsp", [K3, 2, SEG], BF16)
        c_seg = sb("c_seg", [P, 2, SEG])
        c_cur = sb("c_cur", [P, SEG])
        ym = sb("ym", [P, 512])
        SLOTS = SEGS * GROUPS + 1
        y_tok = sb("y_tok", [P, TILES, SLOTS * HG])

        xp = sb("xp", [P, 2, TT, DM])
        stat = sb("stat", [P, TT, 6])
        pause = sb("pause", [P, 2])
        mv = sb("mv", [P, TT, 2])
        vpe = sb("vpe", [P, TT])
        rstd = sb("rstd", [P, TT])
        xn = sb("xn", [P, TT, DM])
        xnt = sb("xnt", [P, 3, 2, SEG])
        res_b = sb("res_b", [P, STEP])
        res_d = sb("res_d", [K3, STEP])
        hi_d = sb("hi_d", [K3, STEP], BF16)
        mid_d = sb("mid_d", [K3, STEP], BF16)

        xe = sb("xe", [P, 2, TT, DM])
        xs = sb("xs", [P, 2, STEP])
        ys = sb("ys", [P, TT, H])
        sg = sb("sg", [P, 2, 512])
        yts = sb("yts", [H, STEP])
        yfull = sb("yfull", [P, 2, STEP])
        tt_f = sb("tt_f", [P, 512])
        prod = sb("prod", [P, 512])
        res = sb("res", [P, 2, TT, DM])

        w_in = [sem(f"w_in{i}") for i in range(9)]
        setup_v, setup_p, setup_pe, setup_a = sem("setup_v"), sem("setup_p"), sem("setup_pe"), sem("setup_a")
        z_ready, exp_done, ln_done = sem("z_ready"), sem("exp_done"), sem("ln_done")
        d_ready, a_ready, b_ready, h_ready = sem("d_ready"), sem("a_ready"), sem("b_ready"), sem("h_ready")
        carry_done, y_ready, y_masked, y_done = sem("carry_done"), sem("y_ready"), sem("y_masked"), sem("y_done")
        c_cur_ready = sem("c_cur_ready")
        x_in = [sem("x_in0"), sem("x_in1")]
        stat_done, aggr_done, vpe_done, rstd_done = sem("stat_done"), sem("aggr_done"), sem("vpe_done"), sem("rstd_done")
        xn_done, xt_ready, xnt_done, proj_ready = sem("xn_done"), sem("xt_ready"), sem("xnt_done"), sem("proj_ready")
        hi_done, res_done, mid_done, split_done = sem("hi_done"), sem("res_done"), sem("mid_done"), sem("split_done")
        xe_in = [sem("xe_in0"), sem("xe_in1")]
        xs_ready, n_ready, nexp_done, nln_done = sem("xs_ready"), sem("n_ready"), sem("nexp_done"), sem("nln_done")
        sp_done, sg_done, silu_done = sem("sp_done"), sem("sg_done"), sem("silu_done")
        ys_ready, yt_ready, yts_done, ybc_ready = sem("ys_ready"), sem("yt_ready"), sem("yts_done"), sem("ybc_ready")
        mix_done, yfull_done, s_ready, prod_done = sem("mix_done"), sem("yfull_done"), sem("s_ready"), sem("prod_done")
        out_done = sem("out_done")
        stored = [sem("stored0"), sem("stored1")]

        x_rows = x.rearrange("b (t p) d -> p (b t) d", p=P)
        out_rows = out.rearrange("b (t p) d -> p (b t) d", p=P)

        block = ctx.enter_context(nc.Block())

        @block.sync
        def _(sp):
            def load_p(T, i, wait):
                if wait:
                    sp.wait_ge(xn_done, T - 1)
                sp.dma_start(xp[:, i, :, :], x_rows[:, bass.ds(TT * T, TT), :]).then_inc(x_in[i], 16)

            def load_e(T, i, wait):
                if wait:
                    sp.wait_ge(out_done, T - 1)
                sp.dma_start(xe[:, i, :, :], x_rows[:, bass.ds(TT * T, TT), :]).then_inc(xe_in[i], 16)

            def store_e(T, i):
                sp.wait_ge(out_done, T + 1)
                sp.dma_start(out_rows[:, bass.ds(TT * T, TT), :], res[:, i, :, :]).then_inc(stored[i], 16)

            sp.sem_inc(stored[0], 16)
            sp.sem_inc(stored[1], 16)
            load_p(0, 0, False)
            load_p(1, 1, False)
            sp.dma_start(wx[:, :, :], Wx.rearrange("(c k) n -> k c n", k=P)).then_inc(w_in[1], 16)
            sp.dma_start(a_in[:, :], A).then_inc(w_in[2], 16)
            sp.dma_start(dp_in[:, :], Dp.rearrange("(h o) -> h o", o=1)).then_inc(w_in[8], 16)
            load_p(2, 0, True)
            load_p(3, 1, True)
            load_p(4, 0, True)
            with sp.Fori(0, 2) as kk:
                for i in range(2):
                    load_p(2 * kk + i + 5, 1 - i, True)
            for i in range(2):
                load_p(9 + i, 1 - i, True)
                load_e(i, i, False)
                store_e(i, i)
            with sp.Fori(3, 5) as kk:
                for i in range(2):
                    load_p(2 * kk + i + 5, 1 - i, True)
                    load_e(2 * kk + i - 4, i, True)
                    store_e(2 * kk + i - 4, i)
            load_p(NSTEPS - 1, 1, True)
            load_e(6, 0, True)
            store_e(6, 0)
            load_e(7, 1, True)
            store_e(7, 1)
            with sp.Fori(6, 10) as kk:
                for i in range(2):
                    load_e(2 * kk + i - 4, i, True)
                    store_e(2 * kk + i - 4, i)
            for i in range(2):
                sp.wait_ge(stored[i], 16 * NSTEPS // 2 + 16)

        @block.gpsimd
        def _(pool):
            def p_rstd(s, k, i):
                T = 4 * s + 2 * k + i
                pool.wait_ge(aggr_done, 2 * T + 2)
                nc.gpsimd.tensor_tensor(vpe[:, :], mv[:, :, 1], eps[:, :], ALU.add).then_inc(vpe_done, 1)
                pool.wait_ge(vpe_done, T + 1)
                nc.gpsimd.tensor_tensor(rstd[:, :], vpe[:, :], half[:, :], ALU.pow).then_inc(rstd_done, 1)

            def e_xs(s, k, i):
                nc.gpsimd.tensor_copy(xs[:, :, :], xnt[:, s % 3, :, bass.ds(STEP * (2 * k + i), STEP)]).then_inc(xs_ready, 1)

            def e_ys(s, k, i, parts):
                pool.wait_ge(y_done, parts + 1)
                nc.gpsimd.tensor_copy(ys[:, :, :], y_tok[:, bass.ds(TT * (2 * k + i), TT), HG + H * s:HG + H * s + H]).then_inc(ys_ready, 1)

            def e_yfull(s, k, i):
                T = 4 * s + 2 * k + i
                pool.wait_ge(mix_done, 2 * T + 2)
                pool.wait_ge(sg_done, T + 1)
                nc.gpsimd.tensor_tensor(yfull[:, :, :], yfull[:, :, :],
                                        sg[:, 0, :].rearrange("p (a t) -> p a t", a=2), ALU.mult).then_inc(yfull_done, 1)

            def e_out(s, k, i):
                T = 4 * s + 2 * k + i
                pool.wait_ge(xe_in[i], 16 * (2 * s + k) + 16)
                pool.wait_ge(prod_done, T + 1)
                pool.wait_ge(stored[i], 16 * (2 * s + k) + 16)
                nc.gpsimd.tensor_tensor(res[:, i, :, :], xe[:, i, :, :],
                                        prod[:, :].rearrange("p (a d) -> p a d", a=TT), ALU.subtract).then_inc(out_done, 1)

            nc.gpsimd.memset(half[:, :], -0.5)
            nc.gpsimd.memset(eps[:, :], LN_EPS).then_inc(setup_p, 1)
            pool.wait_ge(setup_p, 1)
            with pool.Fori(0, 2) as k:
                for i in range(2):
                    p_rstd(0, k, i)
            for s in range(SEGS):
                with pool.Fori(0, 2) as k:
                    for i in range(2):
                        G = 4 * s + 2 * k + i
                        if s > 0:
                            e_xs(s - 1, k, i)
                        for j in range(HG):
                            U = HG * G + j
                            pool.wait_ge(d_ready, U + 3)
                            nc.gpsimd.tensor_tensor(b_sb[:, j % 2, :], d_sb[:, j % 2, :], d_sb[:, j % 2, :],
                                                    ALU.mult).then_inc(b_ready, 1)
                            if j == 0 and s + 1 < SEGS:
                                p_rstd(s + 1, k, i)
                            if j == 4 and s > 0:
                                e_ys(s - 1, k, i, 4 * G + PARTS)
                            if j == 6 and s > 0:
                                e_yfull(s - 1, k, i)
                        if s % 2 == 0:
                            pool.wait_ge(h_ready, HG * G + HG + 1)
                            nc.gpsimd.tensor_copy(carry[:, bass.ds(HG * (2 * k + i), HG)],
                                                  hs[:, i, :, SEG - 1]).then_inc(carry_done, 1)
                        if s > 0:
                            e_out(s - 1, k, i)
            with pool.Fori(0, 2) as k:
                for i in range(2):
                    e_xs(SEGS - 1, k, i)
                    e_ys(SEGS - 1, k, i, PARTS * (SEGS * GROUPS + 1))
                    e_yfull(SEGS - 1, k, i)
                    e_out(SEGS - 1, k, i)

        @block.scalar
        def _(act):
            def p_xnt(s, k, i):
                T = 4 * s + 2 * k + i
                act.wait_ge(xt_ready, T + 1)
                nc.scalar.activation(xnt[:, s % 3, :, bass.ds(STEP * (2 * k + i), STEP)],
                                     m0[:, :].rearrange("p (a t) -> p a t", a=2), ACT.Copy).then_inc(xnt_done, 1)

            def p_hi(s, k, i):
                T = 4 * s + 2 * k + i
                cols = bass.ds(STEP * (2 * k + i), STEP)
                act.wait_ge(proj_ready, T + 1)
                nc.scalar.activation(bsp[:, s % 2, 0, cols], m12[:, 0, 0:STEP], ACT.Copy)
                nc.scalar.activation(hi_d[:, :], m12[0:K3, 1, 0:STEP], ACT.Copy)
                nc.scalar.activation(c_seg[:, s % 2, cols], m12[:, 0, STEP:2 * STEP], ACT.Copy).then_inc(hi_done, 1)

            def p_mid(s, k, i):
                T = 4 * s + 2 * k + i
                act.wait_ge(res_done, T + 2)
                nc.scalar.activation(bsp[:, s % 2, 1, bass.ds(STEP * (2 * k + i), STEP)], res_b[:, :], ACT.Copy)
                nc.scalar.activation(mid_d[:, :], res_d[:, :], ACT.Copy).then_inc(mid_done, 1)

            def e_exp(s, k, i):
                act.wait_ge(n_ready, 4 * s + 2 * k + i + 1)
                nc.scalar.activation(sg[:, :, :], m12[:, :, :], ACT.Exp).then_inc(nexp_done, 1)

            def e_ln(s, k, i):
                act.wait_ge(nexp_done, 4 * s + 2 * k + i + 1)
                nc.scalar.activation(sg[:, :, :], sg[:, :, :], ACT.Ln, bias=1.0).then_inc(nln_done, 1)

            def e_sg(s, k, i):
                act.wait_ge(sp_done, 4 * s + 2 * k + i + 1)
                nc.scalar.activation(sg[:, :, :], sg[:, :, :], ACT.Exp, scale=-1.0).then_inc(sg_done, 1)

            def e_yts(s, k, i):
                act.wait_ge(yt_ready, 4 * s + 2 * k + i + 1)
                nc.scalar.activation(yts[:, :], m0[0:H, 0:STEP], ACT.Copy).then_inc(yts_done, 1)

            act.dma_start(cst[:, :], consts).then_inc(w_in[0], 16)
            act.dma_start(xs_w := yfull[:, :, :], Wf.rearrange("(c o) i -> o c i", o=P)).then_inc(w_in[3], 16)
            act.dma_start(wgn[:, :, :], Wg.rearrange("(c k) n -> k c n", k=P)).then_inc(w_in[4], 16)
            act.dma_start(wo[:, :, :], Wo.rearrange("(c k) n -> k c n", k=P)).then_inc(w_in[5], 16)
            act.dma_start(rows[:, 0, :], bg.rearrange("(o d) -> o d", o=1)).then_inc(w_in[6], 16)
            act.dma_start(rows[:, 1, :], bf.rearrange("(o d) -> o d", o=1)).then_inc(w_in[7], 16)
            act.wait_ge(w_in[3], 16)
            nc.scalar.activation(prod[:, :], xs_w.rearrange("p a b -> p (a b)"), ACT.Abs).then_inc(setup_a, 1)
            act.wait_ge(setup_pe, 1)
            nc.scalar.activation(a_t[:, :], z_ps[:, 0, 0:H], ACT.Copy).then_inc(setup_a, 1)
            nc.scalar.activation(dp[:, :], z_ps[:, 0, H:H + 2], ACT.Copy).then_inc(setup_a, 1)
            with act.Fori(0, 2) as k:
                for i in range(2):
                    p_xnt(0, k, i)
                    p_hi(0, k, i)
                    p_mid(0, k, i)
            act.wait_ge(setup_pe, 3)
            nc.scalar.activation(wfn[:, :, :], z_ps[:, 1, 0:512].rearrange("p (a o) -> p a o", a=2),
                                 ACT.Copy, scale=-1.0).then_inc(setup_a, 1)

            def unit_a(G, g, j):
                act.wait_ge(d_ready, HG * G + j + 3)
                nc.scalar.activation(a_sb[:, j % 2, :], d_sb[:, j % 2, :], ACT.Exp,
                                     scale=a_t[:, bass.ds(HG * g + j, 1)]).then_inc(a_ready, 1)

            for s in range(SEGS):
                with act.Fori(0, 2) as k:
                    for i in range(2):
                        g = 2 * k + i
                        G = 4 * s + g
                        has_p, has_e = s + 1 < SEGS, s > 0
                        for j in range(HG):
                            U = HG * G + j
                            act.wait_ge(z_ready, U + 1)
                            nc.scalar.activation(e_sb[:, j % 2, :], z_ps[:, j % 2, :], ACT.Exp).then_inc(exp_done, 1)
                            act.wait_ge(exp_done, U + 1)
                            nc.scalar.activation(e_sb[:, j % 2, :], e_sb[:, j % 2, :], ACT.Ln, bias=1.0).then_inc(ln_done, 1)
                            if j > 0:
                                unit_a(G, g, j - 1)
                            if j == 2 and has_p:
                                p_xnt(s + 1, k, i)
                            if j == 1 and has_e:
                                e_exp(s - 1, k, i)
                            if j == 2 and has_e:
                                e_ln(s - 1, k, i)
                            if j == 3 and has_e:
                                e_sg(s - 1, k, i)
                            if j == 5 and has_p:
                                p_hi(s + 1, k, i)
                            if j == 5 and has_e:
                                e_yts(s - 1, k, i)
                            if j == 6 and has_p:
                                p_mid(s + 1, k, i)
                        unit_a(G, g, HG - 1)
            with act.Fori(0, 2) as k:
                for i in range(2):
                    e_exp(SEGS - 1, k, i)
                    e_ln(SEGS - 1, k, i)
                    e_sg(SEGS - 1, k, i)
                    e_yts(SEGS - 1, k, i)

        @block.vector
        def _(dve):
            vs = [0]

            def own(ins):
                vs[0] += 1
                ins.then_inc(setup_v, 1)
                dve.wait_ge(setup_v, vs[0])

            def p_stats(s, k, i):
                T = 4 * s + 2 * k + i
                dve.wait_ge(x_in[i], 16 * (2 * s + k) + 16)
                for t in range(TT):
                    nc.vector.bn_stats(stat[:, t, :], xp[:, i, t, :]).then_inc(stat_done, 1)
                dve.wait_ge(stat_done, TT * T + TT)
                nc.vector.memset(pause[:, :], 0.0)
                for t in range(TT):
                    nc.vector.bn_aggr(mv[:, t, :], stat[:, t, :]).then_inc(aggr_done, 1)

            def p_norm(s, k, i):
                T = 4 * s + 2 * k + i
                dve.wait_ge(rstd_done, T + 1)
                for t in range(TT):
                    ins = nc.vector.tensor_scalar(xn[:, t, :], xp[:, i, t, :], mv[:, t, 0:1], rstd[:, t:t + 1],
                                                  ALU.subtract, ALU.mult)
                ins.then_inc(xn_done, 1)

            def p_res(s, k, i):
                dve.wait_ge(hi_done, 4 * s + 2 * k + i + 1)
                nc.vector.tensor_tensor(res_b[:, :], m12[:, 0, 0:STEP],
                                        bsp[:, s % 2, 0, bass.ds(STEP * (2 * k + i), STEP)], ALU.subtract)
                nc.vector.scalar_tensor_tensor(res_d[:, :], hi_d[:, :], cst[0:K3, C_KEEP:C_KEEP + 1],
                                               m12[0:K3, 1, 0:STEP], ALU.mult, ALU.add).then_inc(res_done, 1)

            def p_low(s, k, i):
                cols = bass.ds(STEP * (2 * k + i), STEP)
                dve.wait_ge(mid_done, 4 * s + 2 * k + i + 1)
                nc.vector.tensor_tensor(bsp[:, s % 2, 2, cols], res_b[:, :], bsp[:, s % 2, 1, cols], ALU.subtract)
                nc.vector.scalar_tensor_tensor(dsp[:, s % 2, cols], mid_d[:, :], cst[0:K3, C_KEEP + 1:C_KEEP + 2],
                                               res_d[:, :], ALU.mult, ALU.add).then_inc(split_done, 1)

            def e_sp(s, k, i):
                dve.wait_ge(nln_done, 4 * s + 2 * k + i + 1)
                nc.vector.scalar_tensor_tensor(sg[:, :, :], sg[:, :, :], SP_CLAMP, m12[:, :, :],
                                               ALU.min, ALU.max).then_inc(sp_done, 1)

            def e_silu(s, k, i):
                dve.wait_ge(sg_done, 4 * s + 2 * k + i + 1)
                nc.vector.tensor_tensor(tt_f[:, :], m12[:, 1, :], sg[:, 1, :], ALU.mult).then_inc(silu_done, 1)

            def e_mix(s, k, i):
                dve.wait_ge(ybc_ready, 4 * s + 2 * k + i + 1)
                for c in range(2):
                    nc.vector.scalar_tensor_tensor(yfull[:, c, :], xs[:, c, :], dp[:, c:c + 1],
                                                   m0[:, STEP * c:STEP * c + STEP], ALU.mult, ALU.add).then_inc(mix_done, 1)

            def e_prod(s, k, i):
                T = 4 * s + 2 * k + i
                dve.wait_ge(s_ready, T + 1)
                dve.wait_ge(silu_done, T + 1)
                nc.vector.tensor_tensor(prod[:, :], m0[:, :], tt_f[:, :], ALU.mult).then_inc(prod_done, 1)

            def y_part(G, p):
                Y = PARTS * G + p
                dve.wait_ge(y_ready, Y + 1)
                dve.wait_ge(y_done, Y + 1)
                nc.vector.tensor_tensor(ym[:, :].rearrange("p (a l) -> p a l", l=BLK),
                                        y_ps[:, :].rearrange("p (a l) -> p a l", l=BLK),
                                        mask[:, None, :].to_broadcast([P, 512 // BLK, BLK]), ALU.mult).then_inc(y_masked, 1)
                dve.wait_ge(y_masked, Y + 2)
                nc.vector.tensor_reduce(y_tok[:, 2 * p:2 * p + 2, bass.ds(HG * G, HG)],
                                        ym[:, :].rearrange("p (t h l) -> p t h l", t=2, l=BLK),
                                        AX_X, ALU.add).then_inc(y_done, 1)

            def unit_d(G, j):
                dve.wait_ge(ln_done, HG * G + j + 1)
                nc.vector.scalar_tensor_tensor(d_sb[:, j % 2, :], e_sb[:, j % 2, :], SP_CLAMP, z_ps[:, j % 2, :],
                                               ALU.min, ALU.max).then_inc(d_ready, 1)

            def unit_scan(s, G, g, j):
                U = HG * G + j
                dve.wait_ge(a_ready, U + 1)
                dve.wait_ge(b_ready, U + 1)
                start = carry[:, bass.ds(HG * g + j, 1)] if s % 2 else 0.0
                nc.vector.tensor_tensor_scan(hs[:, G_PAR[0], j, :], a_sb[:, j % 2, :], b_sb[:, j % 2, :], start,
                                             ALU.mult, ALU.add).then_inc(h_ready, 1)

            G_PAR = [0]
            dve.sem_inc(res_done, 1)
            nc.vector.memset(hs[:, 1, :, :], 0.0)
            nc.vector.memset(c_cur[:, :], 0.0)
            own(nc.vector.memset(ones[:, :], 1.0))
            dve.wait_ge(w_in[0], 16)
            nc.vector.tensor_copy(ident_bf[:, :], ident)
            own(nc.vector.tensor_copy(sel[:, :, :], cst[:, C_EYE:C_EYE + H, None].to_broadcast([P, H, P])))
            dve.wait_ge(w_in[1], 16)
            for r in range(3):
                ins = nc.vector.tensor_copy(wdb[:, :, r, :], wx[:, :, 2 * N:2 * N + H])
            own(ins)
            SETUP_A = vs[0]
            assert SETUP_A == 3
            with dve.Fori(0, 2) as k:
                for i in range(2):
                    p_stats(0, k, i)
                    p_norm(0, k, i)
                    p_res(0, k, i)
                    p_low(0, k, i)
            wf = yfull[:, :, :].rearrange("p a b -> p (a b)")
            dve.wait_ge(setup_a, 1)
            own(nc.vector.reduce_sum(wstat[:, 0:1], prod[:, :], AX_X))
            dve.wait_ge(setup_pe, 2)
            own(nc.vector.tensor_scalar(wstat[:, 1:2], z_ps[:, 1, 0:1], 1.0 / (DM * DM), None, ALU.mult))
            own(nc.vector.tensor_scalar(wstat[:, 2:3], wstat[:, 1:2], W_EPS, None, ALU.add))
            nc.vector.tensor_scalar(wstat[:, 3:4], wstat[:, 2:3], 0.5, None, ALU.mult)
            own(nc.vector.tensor_scalar(wstat[:, 4:5], wstat[:, 2:3], -0.5, None, ALU.mult))
            nc.vector.tensor_scalar(tt_f[:, :], wf, wstat[:, 3:4], None, ALU.is_gt)
            own(nc.vector.tensor_scalar(prod[:, :], wf, wstat[:, 4:5], None, ALU.is_lt))
            own(nc.vector.tensor_tensor(tt_f[:, :], tt_f[:, :], prod[:, :], ALU.subtract))
            own(nc.vector.scalar_tensor_tensor(prod[:, :], tt_f[:, :], wstat[:, 1:2], wf, ALU.mult, ALU.subtract))
            own(nc.vector.tensor_tensor(tt_f[:, :], wf, prod[:, :], ALU.add))
            dve.wait_ge(w_in[4], 16)
            own(nc.vector.tensor_scalar(wgn[:, :, :], wgn[:, :, :], -1.0, None, ALU.mult))
            dve.wait_ge(w_in[6], 16)
            dve.wait_ge(w_in[7], 16)
            own(nc.vector.tensor_scalar(rows[:, :, :], rows[:, :, :], -1.0, None, ALU.mult))
            assert vs[0] == SETUP_V_END
            dve.sem_inc(d_ready, 2)
            dve.sem_inc(h_ready, 1)
            dve.sem_inc(y_masked, 1)
            dve.sem_inc(y_done, 1)

            for s in range(SEGS):
                if s % 2:
                    dve.wait_ge(carry_done, 4 * (s // 2) + 4)
                with dve.Fori(0, 2) as k:
                    for i in range(2):
                        g = 2 * k + i
                        G = 4 * s + g
                        G_PAR[0] = i
                        has_p, has_e = s + 1 < SEGS, s > 0
                        for j in range(HG):
                            unit_d(G, j)
                            if j > 0:
                                unit_scan(s, G, g, j - 1)
                            if 1 <= j <= PARTS:
                                y_part(G, j - 1)
                            if j == PARTS and i == 0:
                                nc.vector.tensor_copy(c_cur[:, :], c_seg[:, s % 2, :]).then_inc(c_cur_ready, 1)
                            if j == 0 and has_p:
                                p_stats(s + 1, k, i)
                            if j == 1 and has_p:
                                p_norm(s + 1, k, i)
                            if j == 3 and has_e:
                                e_sp(s - 1, k, i)
                            if j == 4 and has_e:
                                e_silu(s - 1, k, i)
                            if j == 6 and has_p:
                                p_res(s + 1, k, i)
                            if j == 6 and has_e:
                                e_mix(s - 1, k, i)
                            if j == 7 and has_p:
                                p_low(s + 1, k, i)
                        unit_scan(s, G, g, HG - 1)
                        if has_e:
                            e_prod(s - 1, k, i)
            for p in range(PARTS):
                y_part(SEGS * GROUPS, p)
            with dve.Fori(0, 2) as k:
                for i in range(2):
                    e_sp(SEGS - 1, k, i)
                    e_silu(SEGS - 1, k, i)
                    e_mix(SEGS - 1, k, i)
                    e_prod(SEGS - 1, k, i)

        @block.tensor
        def _(pe):
            def unit_z(s, G, g, j):
                pe.wait_ge(d_ready, HG * G + j + 1)
                if j == 0:
                    pe.wait_ge(split_done, 4 * s + 4)
                for r in range(3):
                    for c in range(2):
                        nc.tensor.matmul(z_ps[:, j % 2, 512 * c:512 * c + 512], ident_bf[:, :],
                                         bsp[:, s % 2, r, 512 * c:512 * c + 512], start=(r == 0), stop=False)
                for c in range(2):
                    ins = nc.tensor.matmul(z_ps[:, j % 2, 512 * c:512 * c + 512], sel[0:K3, HG * g + j, :],
                                           dsp[:, s % 2, 512 * c:512 * c + 512], start=False, stop=True)
                ins.then_inc(z_ready, 1)

            def y_part(G, i, p):
                Y = PARTS * G + p
                if p == 0:
                    pe.wait_ge(h_ready, HG * G + 1)
                pe.wait_ge(y_masked, Y + 1)
                for q in range(2):
                    for c in range(4):
                        t0 = 256 * p + P * q + BLK * c
                        ins = nc.tensor.matmul(y_ps[BLK * c:BLK * c + BLK, 256 * q:256 * q + 256],
                                               c_cur[:, t0:t0 + BLK], hs[:, 1 - i, :, t0:t0 + BLK], start=True, stop=True)
                ins.then_inc(y_ready, 1)

            def p_xt(s, k, i, e_before):
                T = 4 * s + 2 * k + i
                pe.wait_ge(xn_done, T + 1)
                if e_before is not None:
                    pe.wait_ge(prod_done, e_before)
                for c in range(2):
                    for t in range(TT):
                        ins = nc.tensor.transpose(m0[:, STEP * c + P * t:STEP * c + P * t + P],
                                                  xn[:, t, P * c:P * c + P], ident)
                ins.then_inc(xt_ready, 1)

            def p_proj(s, k, i, e_before):
                T = 4 * s + 2 * k + i
                cols = bass.ds(STEP * (2 * k + i), STEP)
                pe.wait_ge(xnt_done, T + 1)
                if e_before is not None:
                    pe.wait_ge(silu_done, e_before)
                pe.wait_ge(res_done, T + 1)
                for o in range(2):
                    for c in range(2):
                        nc.tensor.matmul(m12[:, 0, STEP * o:STEP * o + STEP], wx[:, c, P * o:P * o + P],
                                         xnt[:, s % 3, c, cols], start=(c == 0), stop=(c == 1))
                for c in range(2):
                    ins = nc.tensor.matmul(m12[0:K3, 1, 0:STEP], wdb[:, c, :, :].rearrange("p r h -> p (r h)"),
                                           xnt[:, s % 3, c, cols], start=(c == 0), stop=(c == 1))
                ins.then_inc(proj_ready, 1)

            def e_n(s, k, i, p_before):
                pe.wait_ge(xs_ready, 4 * s + 2 * k + i + 1)
                pe.wait_ge(res_done, p_before + 1)
                for o in range(2):
                    dst = m12[:, 0, STEP * o:STEP * o + STEP]
                    for c in range(2):
                        nc.tensor.matmul(dst, wgn[:, c, P * o:P * o + P], xs[:, c, :], start=(c == 0), stop=False)
                    nc.tensor.matmul(dst, rows[0:1, 0, P * o:P * o + P], ones[0:1, 0:STEP], start=False, stop=True)
                for t in range(TT):
                    dst = m12[:, 1, DM * t:DM * t + DM]
                    for c in range(2):
                        nc.tensor.matmul(dst, xs[:, c, P * t:P * t + P], wfn[:, c, :], start=(c == 0), stop=False)
                    ins = nc.tensor.matmul(dst, ones[0:1, 0:P], rows[0:1, 1, :], start=False, stop=True)
                ins.then_inc(n_ready, 1)

            def e_yt(s, k, i, p_now):
                pe.wait_ge(ys_ready, 4 * s + 2 * k + i + 1)
                pe.wait_ge(xnt_done, p_now)
                for t in range(TT):
                    ins = nc.tensor.transpose(m0[0:H, P * t:P * t + P], ys[:, t, :], ident)
                ins.then_inc(yt_ready, 1)

            def e_ybc(s, k, i):
                pe.wait_ge(yts_done, 4 * s + 2 * k + i + 1)
                for c in range(2):
                    ins = nc.tensor.matmul(m0[:, STEP * c:STEP * c + STEP], cst[0:H, C_REP + P * c:C_REP + P * c + P],
                                           yts[:, :], start=True, stop=True)
                ins.then_inc(ybc_ready, 1)

            def e_s(s, k, i):
                pe.wait_ge(yfull_done, 4 * s + 2 * k + i + 1)
                for t in range(TT):
                    for c in range(2):
                        ins = nc.tensor.matmul(m0[:, DM * t:DM * t + DM], yfull[:, c, P * t:P * t + P], wo[:, c, :],
                                               start=(c == 0), stop=(c == 1))
                ins.then_inc(s_ready, 1)

            pe.wait_ge(w_in[0], 16)
            pe.wait_ge(w_in[2], 16)
            pe.wait_ge(w_in[8], 16)
            nc.tensor.transpose(z_ps[:, 0, 0:H], a_in[:, :], ident[0:H, 0:H])
            for c in range(2):
                ins = nc.tensor.matmul(z_ps[:, 0, H + c:H + c + 1], cst[0:H, C_REP + P * c:C_REP + P * c + P],
                                       dp_in[:, :], start=True, stop=True)
            ins.then_inc(setup_pe, 1)
            pe.wait_ge(setup_v, 3)
            with pe.Fori(0, 2) as k:
                for i in range(2):
                    p_xt(0, k, i, None)
                    p_proj(0, k, i, None)
            pe.wait_ge(setup_v, 4)
            nc.tensor.matmul(z_ps[:, 1, 0:1], ones[:, 0:P], wstat[:, 0:1], start=True, stop=True).then_inc(setup_pe, 1)
            pe.wait_ge(setup_v, SETUP_V_WF)
            for c in range(2):
                for o in range(2):
                    ins = nc.tensor.transpose(z_ps[:, 1, DM * c + P * o:DM * c + P * o + P],
                                              tt_f[:, DM * o + P * c:DM * o + P * c + P], ident)
            ins.then_inc(setup_pe, 1)
            pe.wait_ge(setup_v, SETUP_V_END)
            pe.wait_ge(setup_a, 4)
            pe.wait_ge(w_in[5], 16)
            for s in range(SEGS):
                with pe.Fori(0, 2) as k:
                    for i in range(2):
                        g = 2 * k + i
                        G = 4 * s + g
                        has_p, has_e = s + 1 < SEGS, s > 0
                        e_before = 4 * (s - 1) + g if has_e else None
                        p_before = 4 * (s + 1) + g if has_p else NSTEPS
                        for j in range(HG):
                            unit_z(s, G, g, j)
                            if i == 1 and j == 1:
                                pe.wait_ge(c_cur_ready, 2 * s + k + 1)
                            if 1 <= j <= PARTS:
                                y_part(G, i, j - 1)
                            if j == 1 and has_e:
                                e_n(s - 1, k, i, p_before)
                            if j == 3 and has_p:
                                p_xt(s + 1, k, i, e_before)
                            if j == 5 and has_p:
                                p_proj(s + 1, k, i, e_before + 1 if has_e else None)
                            if j == 5 and has_e:
                                e_yt(s - 1, k, i, p_before + 1 if has_p else NSTEPS)
                            if j == 6 and has_e:
                                e_ybc(s - 1, k, i)
                            if j == 7 and has_e:
                                e_s(s - 1, k, i)
            for p in range(PARTS):
                y_part(SEGS * GROUPS, 0, p)
            with pe.Fori(0, 2) as k:
                for i in range(2):
                    e_n(SEGS - 1, k, i, NSTEPS)
                    e_yt(SEGS - 1, k, i, NSTEPS)
                    e_ybc(SEGS - 1, k, i)
                    e_s(SEGS - 1, k, i)


SETUP_V_WF, SETUP_V_END = 11, 13

_INS = ["L0_attn_x", "L0_attn_Wx", "L0_attn_Wg", "L0_attn_bg", "L0_attn_Wo", "L0_attn_A", "L0_attn_Dp",
        "L0_ffn_weight", "L0_ffn_bias"]


def kernel(**inputs):
    import concourse.bacc as _bacc
    from concourse.bass_utils import run_bass_kernel_spmd as _run

    nc = _bacc.Bacc("TRN2", target_bir_lowering=False, num_devices=1)
    arrays, args = {}, []
    for name in _INS:
        a = np.ascontiguousarray(inputs[name])
        arrays[name] = a
        args.append(nc.dram_tensor(name, a.shape, mybir.dt.from_np(a.dtype), kind="ExternalInput").ap())
    heads, dm = arrays["L0_attn_A"].shape[0], arrays["L0_attn_x"].shape[2]
    arrays["shape_constants"] = shape_constants(heads, dm)
    args.append(nc.dram_tensor("shape_constants", (P, C_COLS), F32, kind="ExternalInput").ap())
    args.append(nc.dram_tensor("out", arrays["L0_attn_x"].shape, F32, kind="ExternalOutput").ap())
    program(nc, *args)
    r = _run(nc, [arrays], core_ids=[0])
    return r.results[0]["out"]
```

```python
from contextlib import ExitStack

import concourse.bass as bass
import numpy as np
from concourse import mybir

F32 = mybir.dt.float32
BF16 = mybir.dt.bfloat16
ALU = mybir.AluOpType
ACT = mybir.ActivationFunctionType
AX_X = mybir.AxisListType.X

P = 128
BLK = 32
STEP = 256
SP_CLAMP = 40.0
LN_EPS = 1e-5
W_EPS = 1e-10

C_ID, C_MASK, C_EYE, C_KEEP, C_KEEP1, C_REP = 0, 128, 160, 192, 194, 196
C_COLS = C_REP + 256


def shape_constants(heads, dm):
    t = np.zeros((P, C_COLS), np.float32)
    row = np.arange(P)
    t[:, C_ID:C_ID + P] = np.eye(P)
    t[:, C_MASK:C_MASK + BLK] = row[:, None] % BLK == np.arange(BLK)
    t[:, C_EYE:C_EYE + heads] = (row[:, None] % heads == np.arange(heads)) & (row[:, None] < 3 * heads)
    t[:, C_KEEP] = np.where(row >= heads, -1.0, 0.0)
    t[:, C_KEEP + 1] = np.where(row >= 2 * heads, -1.0, 0.0)
    t[:, C_KEEP1] = np.where(row >= 1, -1.0, 0.0)
    t[:, C_KEEP1 + 1] = np.where(row >= 2, -1.0, 0.0)
    t[:heads, C_REP:C_REP + dm] = np.arange(dm) // (dm // heads) == np.arange(heads)[:, None]
    return t


def program(nc, x, Wx, Wg, bg, Wo, A, Dp, Wf, bf, consts, out):
    batch, length, DM = x.shape
    H, N = A.shape
    assert N == P and DM == 2 * P and H == 32 and Wx.shape[1] == 2 * N + H
    TOK = batch * length
    SEG = 1024
    SEGS = TOK // SEG
    SEGS_PER_ROW = length // SEG
    assert SEGS == 4 and SEGS_PER_ROW == 2
    HG = 8
    GROUPS = H // HG
    STEPS = SEG // STEP
    assert STEPS == GROUPS == 4
    TT = STEP // P
    TILES = SEG // P
    PARTS = 4
    NSTEPS = SEGS * STEPS
    K3 = 3 * H

    with ExitStack() as ctx:
        def sb(name, shape, dt=F32):
            return ctx.enter_context(nc.sbuf_tensor(name, shape, dt))

        def ps(name, shape):
            return ctx.enter_context(nc.psum_tensor(name, shape, F32))

        def sem(name):
            return ctx.enter_context(nc.semaphore(name))

        z_ps = ps("z_ps", [P, 2, SEG])
        y_ps = ps("y_ps", [P, 512])
        m0 = ps("m0", [P, 512])
        m12 = ps("m12", [P, 2, 512])

        cst = sb("cst", [P, C_COLS])
        ident = cst[:, C_ID:C_ID + P]
        mask = cst[:, C_MASK:C_MASK + BLK]
        ident_bf = sb("ident_bf", [P, P], BF16)
        sel = sb("sel", [P, H, P], BF16)
        wx = sb("wx", [P, 2, 2 * N + H])
        wdb = sb("wdb", [P, 2, 3, H])
        wgn = sb("wgn", [P, 2, DM])
        wo = sb("wo", [P, 2, DM])
        wfn = sb("wfn", [P, 2, DM])
        rows = sb("rows", [3, 2, DM])
        rows_hi = sb("rows_hi", [3, 2, DM], BF16)
        rows_bf = sb("rows_bf", [3, 2, DM], BF16)
        ones = sb("ones", [P, P])
        ones_bf = sb("ones_bf", [3, STEP], BF16)
        dp_in = sb("dp_in", [H, 1])
        dp = sb("dp", [P, 2])
        dp_diag = sb("dp_diag", [P, 2, P])
        a_in = sb("a_in", [H, P])
        a_t = sb("a_t", [P, H])
        half = sb("half", [P, TT])
        eps = sb("eps", [P, TT])
        wstat = sb("wstat", [P, 8])

        e_sb = sb("e_sb", [P, 2, SEG])
        d_sb = sb("d_sb", [P, 2, SEG])
        a_sb = sb("a_sb", [P, 2, SEG])
        b_sb = sb("b_sb", [P, 2, SEG])
        hs = sb("hs", [P, 2, HG, SEG])
        carry = sb("carry", [P, H])
        bsp = sb("bsp", [P, 2, 3, SEG], BF16)
        dsp = sb("dsp", [K3, 2, SEG], BF16)
        c_seg = sb("c_seg", [P, 2, SEG])
        c_cur = sb("c_cur", [P, SEG])
        ym = sb("ym", [P, 512])
        SLOTS = SEGS * GROUPS + 1
        y_tok = sb("y_tok", [P, TILES, SLOTS * HG])

        xp = sb("xp", [P, 2, TT, DM])
        stat = sb("stat", [P, TT, 6])
        pause = sb("pause", [P, 2])
        mv = sb("mv", [P, TT, 2])
        vpe = sb("vpe", [P, TT])
        rstd = sb("rstd", [P, TT])
        xn = sb("xn", [P, TT, DM])
        xnt = sb("xnt", [P, 3, 2, SEG])
        res_b = sb("res_b", [P, STEP])
        res_d = sb("res_d", [K3, STEP])
        hi_d = sb("hi_d", [K3, STEP], BF16)
        mid_d = sb("mid_d", [K3, STEP], BF16)

        xe = sb("xe", [P, 2, TT, DM])
        xs = sb("xs", [P, 2, STEP])
        ys = sb("ys", [P, TT, H, DM // H])
        sg = sb("sg", [P, 2, 512])
        yfull = sb("yfull", [P, 2, STEP])
        tt_f = sb("tt_f", [P, 512])
        prod = sb("prod", [P, 512])

        w_in = [sem(f"w_in{i}") for i in range(9)]
        setup_v, setup_p, setup_pe, setup_a = sem("setup_v"), sem("setup_p"), sem("setup_pe"), sem("setup_a")
        z_ready, exp_done, ln_done = sem("z_ready"), sem("exp_done"), sem("ln_done")
        d_ready, a_ready, b_ready, h_ready = sem("d_ready"), sem("a_ready"), sem("b_ready"), sem("h_ready")
        carry_done, y_ready, y_masked, y_done = sem("carry_done"), sem("y_ready"), sem("y_masked"), sem("y_done")
        c_cur_ready = sem("c_cur_ready")
        x_in = [sem("x_in0"), sem("x_in1")]
        stat_done, aggr_done, vpe_done, rstd_done = sem("stat_done"), sem("aggr_done"), sem("vpe_done"), sem("rstd_done")
        xn_done, xt_ready, xnt_done, proj_ready = sem("xn_done"), sem("xt_ready"), sem("xnt_done"), sem("proj_ready")
        hi_done, res_done, mid_done, split_done = sem("hi_done"), sem("res_done"), sem("mid_done"), sem("split_done")
        xe_in = [sem("xe_in0"), sem("xe_in1")]
        xs_ready, n_ready, nexp_done, nln_done = sem("xs_ready"), sem("n_ready"), sem("nexp_done"), sem("nln_done")
        sp_done, sg_done, silu_done = sem("sp_done"), sem("sg_done"), sem("silu_done")
        ys_ready, mix_ready = sem("ys_ready"), sem("mix_ready")
        yfull_done, s_ready, prod_done = sem("yfull_done"), sem("s_ready"), sem("prod_done")
        out_done = sem("out_done")
        stored = [sem("stored0"), sem("stored1")]

        x_rows = x.rearrange("b (t p) d -> p (b t) d", p=P)
        out_rows = out.rearrange("b (t p) d -> p (b t) d", p=P)

        block = ctx.enter_context(nc.Block())

        @block.sync
        def _(sp):
            def load_p(T, i, wait):
                if wait:
                    sp.wait_ge(xn_done, T - 1)
                sp.dma_start(xp[:, i, :, :], x_rows[:, bass.ds(TT * T, TT), :]).then_inc(x_in[i], 16)

            def load_e(T, i, pair, wait):
                if wait:
                    sp.wait_ge(stored[i], 16 * pair)
                sp.dma_start(xe[:, i, :, :], x_rows[:, bass.ds(TT * T, TT), :]).then_inc(xe_in[i], 16)

            def store_e(T, i):
                sp.wait_ge(out_done, T + 1)
                sp.dma_start(out_rows[:, bass.ds(TT * T, TT), :], xe[:, i, :, :]).then_inc(stored[i], 16)

            load_p(0, 0, False)
            load_p(1, 1, False)
            sp.dma_start(wx[:, :, :], Wx.rearrange("(c k) n -> k c n", k=P)).then_inc(w_in[1], 16)
            sp.dma_start(a_in[:, :], A).then_inc(w_in[2], 16)
            sp.dma_start(dp_in[:, :], Dp.rearrange("(h o) -> h o", o=1)).then_inc(w_in[8], 16)
            load_p(2, 0, True)
            load_p(3, 1, True)
            load_p(4, 0, True)
            with sp.Fori(0, 2) as kk:
                for i in range(2):
                    load_p(2 * kk + i + 5, 1 - i, True)
            for i in range(2):
                load_p(9 + i, 1 - i, True)
                load_e(i, i, 0, False)
                store_e(i, i)
            with sp.Fori(3, 5) as kk:
                for i in range(2):
                    load_p(2 * kk + i + 5, 1 - i, True)
                    load_e(2 * kk + i - 4, i, kk - 2, True)
                    store_e(2 * kk + i - 4, i)
            load_p(NSTEPS - 1, 1, True)
            load_e(6, 0, 3, True)
            store_e(6, 0)
            load_e(7, 1, 3, True)
            store_e(7, 1)
            with sp.Fori(6, 10) as kk:
                for i in range(2):
                    load_e(2 * kk + i - 4, i, kk - 2, True)
                    store_e(2 * kk + i - 4, i)
            for i in range(2):
                sp.wait_ge(stored[i], 16 * NSTEPS // 2)

        @block.gpsimd
        def _(pool):
            def p_rstd(s, k, i):
                T = 4 * s + 2 * k + i
                pool.wait_ge(aggr_done, 2 * T + 2)
                nc.gpsimd.tensor_tensor(vpe[:, :], mv[:, :, 1], eps[:, :], ALU.add).then_inc(vpe_done, 1)
                pool.wait_ge(vpe_done, T + 1)
                nc.gpsimd.tensor_tensor(rstd[:, :], vpe[:, :], half[:, :], ALU.pow).then_inc(rstd_done, 1)

            def e_xs(s, k, i):
                nc.gpsimd.tensor_copy(xs[:, :, :], xnt[:, s % 3, :, bass.ds(STEP * (2 * k + i), STEP)]).then_inc(xs_ready, 1)

            def e_out(s, k, i):
                T = 4 * s + 2 * k + i
                pool.wait_ge(xe_in[i], 16 * (2 * s + k) + 16)
                pool.wait_ge(prod_done, T + 1)
                nc.gpsimd.tensor_tensor(xe[:, i, :, :], xe[:, i, :, :],
                                        prod[:, :].rearrange("p (a d) -> p a d", a=TT), ALU.subtract).then_inc(out_done, 1)

            nc.gpsimd.memset(half[:, :], -0.5)
            nc.gpsimd.memset(eps[:, :], LN_EPS).then_inc(setup_p, 1)
            pool.wait_ge(setup_p, 1)
            with pool.Fori(0, 2) as k:
                for i in range(2):
                    p_rstd(0, k, i)
            for s in range(SEGS):
                with pool.Fori(0, 2) as k:
                    for i in range(2):
                        G = 4 * s + 2 * k + i
                        if s > 0:
                            e_xs(s - 1, k, i)
                        for j in range(HG):
                            U = HG * G + j
                            pool.wait_ge(d_ready, U + 3)
                            nc.gpsimd.tensor_tensor(b_sb[:, j % 2, :], d_sb[:, j % 2, :], d_sb[:, j % 2, :],
                                                    ALU.mult).then_inc(b_ready, 1)
                            if j == 0 and s + 1 < SEGS:
                                p_rstd(s + 1, k, i)
                            if j == 5 and i == 0:
                                nc.gpsimd.tensor_scalar(c_cur[:, :], c_seg[:, s % 2, :], 1.0, 0.0, ALU.mult,
                                                        ALU.add).then_inc(c_cur_ready, 1)
                        if s % 2 == 0:
                            pool.wait_ge(h_ready, HG * G + HG + 1)
                            nc.gpsimd.tensor_copy(carry[:, bass.ds(HG * (2 * k + i), HG)],
                                                  hs[:, i, :, SEG - 1]).then_inc(carry_done, 1)
                        if s > 0:
                            e_out(s - 1, k, i)
            with pool.Fori(0, 2) as k:
                for i in range(2):
                    e_xs(SEGS - 1, k, i)
                    e_out(SEGS - 1, k, i)

        @block.scalar
        def _(act):
            def p_xnt(s, k, i):
                T = 4 * s + 2 * k + i
                act.wait_ge(xt_ready, T + 1)
                nc.scalar.activation(xnt[:, s % 3, :, bass.ds(STEP * (2 * k + i), STEP)],
                                     m0[:, :].rearrange("p (a t) -> p a t", a=2), ACT.Copy).then_inc(xnt_done, 1)

            def p_hi(s, k, i):
                T = 4 * s + 2 * k + i
                cols = bass.ds(STEP * (2 * k + i), STEP)
                act.wait_ge(proj_ready, T + 1)
                nc.scalar.activation(bsp[:, s % 2, 0, cols], m12[:, 0, 0:STEP], ACT.Copy)
                nc.scalar.activation(hi_d[:, :], m12[0:K3, 1, 0:STEP], ACT.Copy)
                nc.scalar.activation(c_seg[:, s % 2, cols], m12[:, 0, STEP:2 * STEP], ACT.Copy).then_inc(hi_done, 1)

            def p_mid(s, k, i):
                T = 4 * s + 2 * k + i
                act.wait_ge(res_done, T + 2)
                nc.scalar.activation(bsp[:, s % 2, 1, bass.ds(STEP * (2 * k + i), STEP)], res_b[:, :], ACT.Copy)
                nc.scalar.activation(mid_d[:, :], res_d[:, :], ACT.Copy).then_inc(mid_done, 1)

            def e_exp(s, k, i):
                act.wait_ge(n_ready, 4 * s + 2 * k + i + 1)
                nc.scalar.activation(sg[:, :, :], m12[:, :, :], ACT.Exp).then_inc(nexp_done, 1)

            def e_ln(s, k, i):
                act.wait_ge(nexp_done, 4 * s + 2 * k + i + 1)
                nc.scalar.activation(sg[:, :, :], sg[:, :, :], ACT.Ln, bias=1.0).then_inc(nln_done, 1)

            def e_sg(s, k, i):
                act.wait_ge(sp_done, 4 * s + 2 * k + i + 1)
                nc.scalar.activation(sg[:, :, :], sg[:, :, :], ACT.Exp, scale=-1.0).then_inc(sg_done, 1)

            nc.scalar.preload_act_table_set("natural_log_exp_and_others")
            act.dma_start(cst[:, :], consts).then_inc(w_in[0], 16)
            act.dma_start(xs_w := yfull[:, :, :], Wf.rearrange("(c o) i -> o c i", o=P)).then_inc(w_in[3], 16)
            act.dma_start(wgn[:, :, :], Wg.rearrange("(c k) n -> k c n", k=P)).then_inc(w_in[4], 16)
            act.dma_start(wo[:, :, :], Wo.rearrange("(c k) n -> k c n", k=P)).then_inc(w_in[5], 16)
            act.dma_start(rows[:, 0, :], bg[None, :].to_broadcast([3, DM])).then_inc(w_in[6], 16)
            act.dma_start(rows[:, 1, :], bf[None, :].to_broadcast([3, DM])).then_inc(w_in[7], 16)
            act.wait_ge(w_in[3], 16)
            nc.scalar.activation(prod[:, :], xs_w.rearrange("p a b -> p (a b)"), ACT.Abs).then_inc(setup_a, 1)
            act.wait_ge(setup_pe, 1)
            nc.scalar.activation(a_t[:, :], z_ps[:, 0, 0:H], ACT.Copy).then_inc(setup_a, 1)
            nc.scalar.activation(dp[:, :], z_ps[:, 0, H:H + 2], ACT.Copy).then_inc(setup_a, 1)
            with act.Fori(0, 2) as k:
                for i in range(2):
                    p_xnt(0, k, i)
                    p_hi(0, k, i)
                    p_mid(0, k, i)
            act.wait_ge(setup_pe, 3)
            nc.scalar.activation(wfn[:, :, :], z_ps[:, 1, 0:512].rearrange("p (a o) -> p a o", a=2),
                                 ACT.Copy, scale=-1.0).then_inc(setup_a, 1)

            def unit_a(G, g, j):
                act.wait_ge(d_ready, HG * G + j + 3)
                nc.scalar.activation(a_sb[:, j % 2, :], d_sb[:, j % 2, :], ACT.Exp,
                                     scale=a_t[:, bass.ds(HG * g + j, 1)]).then_inc(a_ready, 1)

            for s in range(SEGS):
                with act.Fori(0, 2) as k:
                    for i in range(2):
                        g = 2 * k + i
                        G = 4 * s + g
                        has_p, has_e = s + 1 < SEGS, s > 0
                        for j in range(HG):
                            U = HG * G + j
                            act.wait_ge(z_ready, U + 1)
                            nc.scalar.activation(e_sb[:, j % 2, :], z_ps[:, j % 2, :], ACT.Exp).then_inc(exp_done, 1)
                            act.wait_ge(exp_done, U + 1)
                            nc.scalar.activation(e_sb[:, j % 2, :], e_sb[:, j % 2, :], ACT.Ln, bias=1.0).then_inc(ln_done, 1)
                            if j > 0:
                                unit_a(G, g, j - 1)
                            if j == 2 and has_e:
                                e_exp(s - 1, k, i)
                            if j == 3 and has_e:
                                e_ln(s - 1, k, i)
                            if j == 4 and has_p:
                                p_xnt(s + 1, k, i)
                            if j == 5 and has_e:
                                e_sg(s - 1, k, i)
                            if j == 7 and has_p:
                                p_hi(s + 1, k, i)
                        unit_a(G, g, HG - 1)
                        if has_p:
                            p_mid(s + 1, k, i)
            with act.Fori(0, 2) as k:
                for i in range(2):
                    e_exp(SEGS - 1, k, i)
                    e_ln(SEGS - 1, k, i)
                    e_sg(SEGS - 1, k, i)

        @block.vector
        def _(dve):
            vs = [0]

            def own(ins):
                vs[0] += 1
                ins.then_inc(setup_v, 1)
                dve.wait_ge(setup_v, vs[0])

            def p_stats(s, k, i):
                T = 4 * s + 2 * k + i
                dve.wait_ge(x_in[i], 16 * (2 * s + k) + 16)
                for t in range(TT):
                    nc.vector.bn_stats(stat[:, t, :], xp[:, i, t, :]).then_inc(stat_done, 1)
                dve.wait_ge(stat_done, TT * T + TT)
                nc.vector.memset(pause[:, :], 0.0)
                for t in range(TT):
                    nc.vector.bn_aggr(mv[:, t, :], stat[:, t, :]).then_inc(aggr_done, 1)

            def p_norm(s, k, i):
                T = 4 * s + 2 * k + i
                dve.wait_ge(rstd_done, T + 1)
                for t in range(TT):
                    ins = nc.vector.tensor_scalar(xn[:, t, :], xp[:, i, t, :], mv[:, t, 0:1], rstd[:, t:t + 1],
                                                  ALU.subtract, ALU.mult)
                ins.then_inc(xn_done, 1)

            def p_res(s, k, i):
                dve.wait_ge(hi_done, 4 * s + 2 * k + i + 1)
                nc.vector.tensor_tensor(res_b[:, :], m12[:, 0, 0:STEP],
                                        bsp[:, s % 2, 0, bass.ds(STEP * (2 * k + i), STEP)], ALU.subtract)
                nc.vector.scalar_tensor_tensor(res_d[:, :], hi_d[:, :], cst[0:K3, C_KEEP:C_KEEP + 1],
                                               m12[0:K3, 1, 0:STEP], ALU.mult, ALU.add).then_inc(res_done, 1)

            def p_low(s, k, i):
                cols = bass.ds(STEP * (2 * k + i), STEP)
                dve.wait_ge(mid_done, 4 * s + 2 * k + i + 1)
                nc.vector.tensor_tensor(bsp[:, s % 2, 2, cols], res_b[:, :], bsp[:, s % 2, 1, cols], ALU.subtract)
                nc.vector.scalar_tensor_tensor(dsp[:, s % 2, cols], mid_d[:, :], cst[0:K3, C_KEEP + 1:C_KEEP + 2],
                                               res_d[:, :], ALU.mult, ALU.add).then_inc(split_done, 1)

            def e_sp(s, k, i):
                dve.wait_ge(nln_done, 4 * s + 2 * k + i + 1)
                nc.vector.scalar_tensor_tensor(sg[:, :, :], sg[:, :, :], SP_CLAMP, m12[:, :, :],
                                               ALU.min, ALU.max).then_inc(sp_done, 1)

            def e_silu(s, k, i):
                dve.wait_ge(sg_done, 4 * s + 2 * k + i + 1)
                nc.vector.tensor_tensor(tt_f[:, :], m12[:, 1, :], sg[:, 1, :], ALU.mult).then_inc(silu_done, 1)

            def e_ys(s, k, i):
                nc.vector.tensor_copy(ys[:, :, :, :],
                                      y_tok[:, bass.ds(TT * (2 * k + i), TT), HG + H * s:HG + H * s + H, None]
                                      .to_broadcast([P, TT, H, DM // H])).then_inc(ys_ready, 1)

            def e_yfull(s, k, i):
                T = 4 * s + 2 * k + i
                dve.wait_ge(mix_ready, T + 1)
                dve.wait_ge(sg_done, T + 1)
                nc.vector.tensor_tensor(yfull[:, :, :].rearrange("p a t -> p (a t)"), m0[:, :], sg[:, 0, :],
                                        ALU.mult).then_inc(yfull_done, 1)

            def e_prod(s, k, i):
                T = 4 * s + 2 * k + i
                dve.wait_ge(s_ready, T + 1)
                dve.wait_ge(silu_done, T + 1)
                nc.vector.tensor_tensor(prod[:, :], m0[:, :], tt_f[:, :], ALU.mult).then_inc(prod_done, 1)

            def y_part(G, p):
                Y = PARTS * G + p
                dve.wait_ge(y_ready, Y + 1)
                dve.wait_ge(y_done, Y + 1)
                nc.vector.tensor_tensor(ym[:, :].rearrange("p (a l) -> p a l", l=BLK),
                                        y_ps[:, :].rearrange("p (a l) -> p a l", l=BLK),
                                        mask[:, None, :].to_broadcast([P, 512 // BLK, BLK]), ALU.mult).then_inc(y_masked, 1)
                dve.wait_ge(y_masked, Y + 2)
                nc.vector.tensor_reduce(y_tok[:, 2 * p:2 * p + 2, bass.ds(HG * G, HG)],
                                        ym[:, :].rearrange("p (t h l) -> p t h l", t=2, l=BLK),
                                        AX_X, ALU.add).then_inc(y_done, 1)

            def unit_d(G, j):
                dve.wait_ge(ln_done, HG * G + j + 1)
                nc.vector.scalar_tensor_tensor(d_sb[:, j % 2, :], e_sb[:, j % 2, :], SP_CLAMP, z_ps[:, j % 2, :],
                                               ALU.min, ALU.max).then_inc(d_ready, 1)

            def unit_scan(s, G, g, j):
                U = HG * G + j
                dve.wait_ge(a_ready, U + 1)
                dve.wait_ge(b_ready, U + 1)
                start = carry[:, bass.ds(HG * g + j, 1)] if s % 2 else 0.0
                nc.vector.tensor_tensor_scan(hs[:, G_PAR[0], j, :], a_sb[:, j % 2, :], b_sb[:, j % 2, :], start,
                                             ALU.mult, ALU.add).then_inc(h_ready, 1)

            G_PAR = [0]
            dve.sem_inc(res_done, 1)
            nc.vector.memset(hs[:, 1, :, :], 0.0)
            nc.vector.memset(c_cur[:, :], 0.0)
            own(nc.vector.memset(ones[:, :], 1.0))
            dve.wait_ge(w_in[0], 16)
            nc.vector.tensor_copy(ident_bf[:, :], ident)
            own(nc.vector.tensor_copy(sel[:, :, :], cst[:, C_EYE:C_EYE + H, None].to_broadcast([P, H, P])))
            dve.wait_ge(w_in[1], 16)
            for r in range(3):
                ins = nc.vector.tensor_copy(wdb[:, :, r, :], wx[:, :, 2 * N:2 * N + H])
            own(ins)
            SETUP_A = vs[0]
            assert SETUP_A == 3
            with dve.Fori(0, 2) as k:
                for i in range(2):
                    p_stats(0, k, i)
                    p_norm(0, k, i)
                    p_res(0, k, i)
                    p_low(0, k, i)
            wf = yfull[:, :, :].rearrange("p a b -> p (a b)")
            dve.wait_ge(setup_a, 1)
            own(nc.vector.reduce_sum(wstat[:, 0:1], prod[:, :], AX_X))
            dve.wait_ge(setup_pe, 2)
            own(nc.vector.tensor_scalar(wstat[:, 1:2], z_ps[:, 1, 0:1], 1.0 / (DM * DM), None, ALU.mult))
            own(nc.vector.tensor_scalar(wstat[:, 2:3], wstat[:, 1:2], W_EPS, None, ALU.add))
            nc.vector.tensor_scalar(wstat[:, 3:4], wstat[:, 2:3], 0.5, None, ALU.mult)
            own(nc.vector.tensor_scalar(wstat[:, 4:5], wstat[:, 2:3], -0.5, None, ALU.mult))
            nc.vector.tensor_scalar(tt_f[:, :], wf, wstat[:, 3:4], None, ALU.is_gt)
            own(nc.vector.tensor_scalar(prod[:, :], wf, wstat[:, 4:5], None, ALU.is_lt))
            own(nc.vector.tensor_tensor(tt_f[:, :], tt_f[:, :], prod[:, :], ALU.subtract))
            own(nc.vector.scalar_tensor_tensor(prod[:, :], tt_f[:, :], wstat[:, 1:2], wf, ALU.mult, ALU.subtract))
            own(nc.vector.tensor_tensor(tt_f[:, :], wf, prod[:, :], ALU.add))
            dve.wait_ge(w_in[4], 16)
            own(nc.vector.tensor_scalar(wgn[:, :, :], wgn[:, :, :], -1.0, None, ALU.mult))
            dve.wait_ge(w_in[6], 16)
            dve.wait_ge(w_in[7], 16)
            own(nc.vector.tensor_scalar(rows[:, :, :], rows[:, :, :], -1.0, None, ALU.mult))
            own(nc.vector.tensor_copy(rows_hi[:, :, :], rows[:, :, :]))
            for part in range(2):
                keep = cst[0:3, C_KEEP1 + part:C_KEEP1 + part + 1]
                dst = (rows, rows_bf)[part]
                own(nc.vector.scalar_tensor_tensor(dst[:, :, :], rows_hi[:, :, :], keep, rows[:, :, :], ALU.mult, ALU.add))
                if part == 0:
                    own(nc.vector.tensor_copy(rows_hi[:, :, :], rows[:, :, :]))
            nc.vector.memset(ones_bf[:, :], 1.0)
            dve.wait_ge(setup_a, 3)
            for c in range(2):
                ins = nc.vector.tensor_scalar(dp_diag[:, c, :], ident, dp[:, c:c + 1], None, ALU.mult)
            own(ins)
            assert vs[0] == SETUP_V_END
            dve.sem_inc(d_ready, 2)
            dve.sem_inc(h_ready, 1)
            dve.sem_inc(y_masked, 1)
            dve.sem_inc(y_done, 1)

            for s in range(SEGS):
                if s % 2:
                    dve.wait_ge(carry_done, 4 * (s // 2) + 4)
                with dve.Fori(0, 2) as k:
                    for i in range(2):
                        g = 2 * k + i
                        G = 4 * s + g
                        G_PAR[0] = i
                        has_p, has_e = s + 1 < SEGS, s > 0
                        for j in range(HG):
                            unit_d(G, j)
                            if j > 0:
                                unit_scan(s, G, g, j - 1)
                            if j < PARTS:
                                y_part(G, j)
                            if j == 0 and has_p:
                                p_stats(s + 1, k, i)
                            if j == 2 and has_p:
                                p_norm(s + 1, k, i)
                            if j == 3 and has_e:
                                e_ys(s - 1, k, i)
                            if j == 4 and has_e:
                                e_sp(s - 1, k, i)
                            if j == 6 and has_e:
                                e_silu(s - 1, k, i)
                                e_yfull(s - 1, k, i)
                            if j == 7 and has_p:
                                p_res(s + 1, k, i)
                        unit_scan(s, G, g, HG - 1)
                        if has_p:
                            p_low(s + 1, k, i)
                        if has_e:
                            e_prod(s - 1, k, i)
            for p in range(PARTS):
                y_part(SEGS * GROUPS, p)
            with dve.Fori(0, 2) as k:
                for i in range(2):
                    e_ys(SEGS - 1, k, i)
                    e_sp(SEGS - 1, k, i)
                    e_silu(SEGS - 1, k, i)
                    e_yfull(SEGS - 1, k, i)
                    e_prod(SEGS - 1, k, i)

        @block.tensor
        def _(pe):
            def unit_z(s, G, g, j):
                pe.wait_ge(d_ready, HG * G + j + 1)
                if j == 0:
                    pe.wait_ge(split_done, 4 * s + 4)
                for r in range(3):
                    for c in range(2):
                        nc.tensor.matmul(z_ps[:, j % 2, 512 * c:512 * c + 512], ident_bf[:, :],
                                         bsp[:, s % 2, r, 512 * c:512 * c + 512], start=(r == 0), stop=False)
                for c in range(2):
                    ins = nc.tensor.matmul(z_ps[:, j % 2, 512 * c:512 * c + 512], sel[0:K3, HG * g + j, :],
                                           dsp[:, s % 2, 512 * c:512 * c + 512], start=False, stop=True)
                ins.then_inc(z_ready, 1)

            def y_part(G, i, p):
                Y = PARTS * G + p
                if p == 0:
                    pe.wait_ge(h_ready, HG * G + 1)
                pe.wait_ge(y_masked, Y + 1)
                for q in range(2):
                    for c in range(4):
                        t0 = 256 * p + P * q + BLK * c
                        ins = nc.tensor.matmul(y_ps[BLK * c:BLK * c + BLK, 256 * q:256 * q + 256],
                                               c_cur[:, t0:t0 + BLK], hs[:, 1 - i, :, t0:t0 + BLK], start=True, stop=True)
                ins.then_inc(y_ready, 1)

            def p_xt(s, k, i, e_before):
                T = 4 * s + 2 * k + i
                pe.wait_ge(xn_done, T + 1)
                if e_before is not None:
                    pe.wait_ge(prod_done, e_before)
                for c in range(2):
                    for t in range(TT):
                        ins = nc.tensor.transpose(m0[:, STEP * c + P * t:STEP * c + P * t + P],
                                                  xn[:, t, P * c:P * c + P], ident)
                ins.then_inc(xt_ready, 1)

            def p_bc(s, k, i, e_now):
                T = 4 * s + 2 * k + i
                cols = bass.ds(STEP * (2 * k + i), STEP)
                pe.wait_ge(xnt_done, T + 1)
                if e_now is not None:
                    pe.wait_ge(sp_done, e_now)
                pe.wait_ge(res_done, T + 1)
                for o in range(2):
                    for c in range(2):
                        nc.tensor.matmul(m12[:, 0, STEP * o:STEP * o + STEP], wx[:, c, P * o:P * o + P],
                                         xnt[:, s % 3, c, cols], start=(c == 0), stop=(c == 1))

            def p_db(s, k, i, e_now):
                cols = bass.ds(STEP * (2 * k + i), STEP)
                if e_now is not None:
                    pe.wait_ge(silu_done, e_now)
                for c in range(2):
                    ins = nc.tensor.matmul(m12[0:K3, 1, 0:STEP], wdb[:, c, :, :].rearrange("p r h -> p (r h)"),
                                           xnt[:, s % 3, c, cols], start=(c == 0), stop=(c == 1))
                ins.then_inc(proj_ready, 1)

            def e_gate(s, k, i, p_before):
                pe.wait_ge(xs_ready, 4 * s + 2 * k + i + 1)
                pe.wait_ge(res_done, p_before + 1)
                for o in range(2):
                    dst = m12[:, 0, STEP * o:STEP * o + STEP]
                    for c in range(2):
                        nc.tensor.matmul(dst, wgn[:, c, P * o:P * o + P], xs[:, c, :], start=(c == 0), stop=False)
                    nc.tensor.matmul(dst, rows_bf[:, 0, P * o:P * o + P], ones_bf[:, :], start=False, stop=True)

            def e_ffn(s, k, i):
                for t in range(TT):
                    dst = m12[:, 1, DM * t:DM * t + DM]
                    for c in range(2):
                        nc.tensor.matmul(dst, xs[:, c, P * t:P * t + P], wfn[:, c, :], start=(c == 0), stop=False)
                    ins = nc.tensor.matmul(dst, ones_bf[:, 0:P], rows_bf[:, 1, :], start=False, stop=True)
                ins.then_inc(n_ready, 1)

            def e_mix(s, k, i, p_now):
                pe.wait_ge(ys_ready, 4 * s + 2 * k + i + 1)
                pe.wait_ge(xnt_done, p_now)
                for c in range(2):
                    dst = m0[:, STEP * c:STEP * c + STEP]
                    nc.tensor.matmul(dst, dp_diag[:, c, :], xs[:, c, :], start=True, stop=False)
                    for t in range(TT):
                        ins = nc.tensor.matmul(dst[:, P * t:P * t + P],
                                               ys[:, t, H // 2 * c:H // 2 * c + H // 2, :].rearrange("p h e -> p (h e)"),
                                               ident, start=False, stop=(t == TT - 1))
                ins.then_inc(mix_ready, 1)

            def e_s(s, k, i):
                pe.wait_ge(yfull_done, 4 * s + 2 * k + i + 1)
                for t in range(TT):
                    for c in range(2):
                        ins = nc.tensor.matmul(m0[:, DM * t:DM * t + DM], yfull[:, c, P * t:P * t + P], wo[:, c, :],
                                               start=(c == 0), stop=(c == 1))
                ins.then_inc(s_ready, 1)

            pe.wait_ge(w_in[0], 16)
            pe.wait_ge(w_in[2], 16)
            pe.wait_ge(w_in[8], 16)
            nc.tensor.transpose(z_ps[:, 0, 0:H], a_in[:, :], ident[0:H, 0:H])
            for c in range(2):
                ins = nc.tensor.matmul(z_ps[:, 0, H + c:H + c + 1], cst[0:H, C_REP + P * c:C_REP + P * c + P],
                                       dp_in[:, :], start=True, stop=True)
            ins.then_inc(setup_pe, 1)
            pe.wait_ge(setup_v, 3)
            with pe.Fori(0, 2) as k:
                for i in range(2):
                    p_xt(0, k, i, None)
                    p_bc(0, k, i, None)
                    p_db(0, k, i, None)
            pe.wait_ge(setup_v, 4)
            nc.tensor.matmul(z_ps[:, 1, 0:1], ones[:, 0:P], wstat[:, 0:1], start=True, stop=True).then_inc(setup_pe, 1)
            pe.wait_ge(setup_v, SETUP_V_WF)
            for c in range(2):
                for o in range(2):
                    ins = nc.tensor.transpose(z_ps[:, 1, DM * c + P * o:DM * c + P * o + P],
                                              tt_f[:, DM * o + P * c:DM * o + P * c + P], ident)
            ins.then_inc(setup_pe, 1)
            pe.wait_ge(setup_v, SETUP_V_END)
            pe.wait_ge(setup_a, 4)
            pe.wait_ge(w_in[5], 16)
            for s in range(SEGS):
                with pe.Fori(0, 2) as k:
                    for i in range(2):
                        g = 2 * k + i
                        G = 4 * s + g
                        has_p, has_e = s + 1 < SEGS, s > 0
                        e_before = 4 * (s - 1) + g if has_e else None
                        p_before = 4 * (s + 1) + g if has_p else NSTEPS
                        for j in range(HG):
                            unit_z(s, G, g, j)
                            if i == 1 and j == 0:
                                pe.wait_ge(c_cur_ready, 2 * s + k + 1)
                            if j < PARTS:
                                y_part(G, i, j)
                            if j == 0 and has_e:
                                e_gate(s - 1, k, i, p_before)
                            if j == 1 and has_e:
                                e_ffn(s - 1, k, i)
                            if j == 4 and has_p:
                                p_xt(s + 1, k, i, e_before)
                            if j == 5 and has_e:
                                e_mix(s - 1, k, i, p_before + 1 if has_p else NSTEPS)
                            if j == 6 and has_p:
                                p_bc(s + 1, k, i, e_before + 1 if has_e else None)
                            if j == 7 and has_p:
                                p_db(s + 1, k, i, e_before + 1 if has_e else None)
                            if j == 7 and has_e:
                                e_s(s - 1, k, i)
            for p in range(PARTS):
                y_part(SEGS * GROUPS, 0, p)
            with pe.Fori(0, 2) as k:
                for i in range(2):
                    e_gate(SEGS - 1, k, i, NSTEPS)
                    e_ffn(SEGS - 1, k, i)
                    e_mix(SEGS - 1, k, i, NSTEPS)
                    e_s(SEGS - 1, k, i)


SETUP_V_WF, SETUP_V_END = 11, 18

_INS = ["L0_attn_x", "L0_attn_Wx", "L0_attn_Wg", "L0_attn_bg", "L0_attn_Wo", "L0_attn_A", "L0_attn_Dp",
        "L0_ffn_weight", "L0_ffn_bias"]


def kernel(**inputs):
    import concourse.bacc as _bacc
    from concourse.bass_utils import run_bass_kernel_spmd as _run

    nc = _bacc.Bacc("TRN2", target_bir_lowering=False, num_devices=1)
    arrays, args = {}, []
    for name in _INS:
        a = np.ascontiguousarray(inputs[name])
        arrays[name] = a
        args.append(nc.dram_tensor(name, a.shape, mybir.dt.from_np(a.dtype), kind="ExternalInput").ap())
    heads, dm = arrays["L0_attn_A"].shape[0], arrays["L0_attn_x"].shape[2]
    arrays["shape_constants"] = shape_constants(heads, dm)
    args.append(nc.dram_tensor("shape_constants", (P, C_COLS), F32, kind="ExternalInput").ap())
    args.append(nc.dram_tensor("out", arrays["L0_attn_x"].shape, F32, kind="ExternalOutput").ap())
    program(nc, *args)
    r = _run(nc, [arrays], core_ids=[0])
    return r.results[0]["out"]
```

```python
from contextlib import ExitStack

import concourse.bass as bass
import numpy as np
from concourse import mybir

F32 = mybir.dt.float32
BF16 = mybir.dt.bfloat16
ALU = mybir.AluOpType
ACT = mybir.ActivationFunctionType
AX_X = mybir.AxisListType.X

P = 128
BLK = 32
STEP = 256
SP_CLAMP = 40.0
LN_EPS = 1e-5
W_EPS = 1e-10

C_ID, C_MASK, C_EYE, C_KEEP, C_KEEP1, C_REP = 0, 128, 160, 192, 194, 196
C_COLS = C_REP + 256


def shape_constants(heads, dm):
    t = np.zeros((P, C_COLS), np.float32)
    row = np.arange(P)
    t[:, C_ID:C_ID + P] = np.eye(P)
    t[:, C_MASK:C_MASK + BLK] = row[:, None] % BLK == np.arange(BLK)
    t[:, C_EYE:C_EYE + heads] = (row[:, None] % heads == np.arange(heads)) & (row[:, None] < 3 * heads)
    t[:, C_KEEP] = np.where(row >= heads, -1.0, 0.0)
    t[:, C_KEEP + 1] = np.where(row >= 2 * heads, -1.0, 0.0)
    t[:, C_KEEP1] = np.where(row >= 1, -1.0, 0.0)
    t[:, C_KEEP1 + 1] = np.where(row >= 2, -1.0, 0.0)
    t[:heads, C_REP:C_REP + dm] = np.arange(dm) // (dm // heads) == np.arange(heads)[:, None]
    return t


def program(nc, x, Wx, Wg, bg, Wo, A, Dp, Wf, bf, consts, out):
    batch, length, DM = x.shape
    H, N = A.shape
    assert N == P and DM == 2 * P and H == 32 and Wx.shape[1] == 2 * N + H
    TOK = batch * length
    SEG = 1024
    SEGS = TOK // SEG
    SEGS_PER_ROW = length // SEG
    assert SEGS == 4 and SEGS_PER_ROW == 2
    HG = 8
    GROUPS = H // HG
    STEPS = SEG // STEP
    assert STEPS == GROUPS == 4
    TT = STEP // P
    TILES = SEG // P
    PARTS = 4
    NSTEPS = SEGS * STEPS
    K3 = 3 * H

    with ExitStack() as ctx:
        def sb(name, shape, dt=F32):
            return ctx.enter_context(nc.sbuf_tensor(name, shape, dt))

        def ps(name, shape):
            return ctx.enter_context(nc.psum_tensor(name, shape, F32))

        def sem(name):
            return ctx.enter_context(nc.semaphore(name))

        z_ps = ps("z_ps", [P, 2, SEG])
        y_ps = ps("y_ps", [P, 512])
        m0 = ps("m0", [P, 512])
        m12 = ps("m12", [P, 2, 512])

        cst = sb("cst", [P, C_COLS])
        ident = cst[:, C_ID:C_ID + P]
        mask = cst[:, C_MASK:C_MASK + BLK]
        ident_bf = sb("ident_bf", [P, P], BF16)
        sel = sb("sel", [P, H, P], BF16)
        wx = sb("wx", [P, 2, 2 * N + H])
        wdb = sb("wdb", [P, 2, 3, H])
        wgn = sb("wgn", [P, 2, DM])
        wo = sb("wo", [P, 2, DM])
        wfn = sb("wfn", [P, 2, DM])
        rows_hi = sb("rows_hi", [3, 2, DM], BF16)
        rows_bf = sb("rows_bf", [3, 2, DM], BF16)
        ones = sb("ones", [P, P])
        ones_bf = sb("ones_bf", [3, STEP], BF16)
        dp_in = sb("dp_in", [H, 1])
        dp = sb("dp", [P, 2])
        dp_diag = sb("dp_diag", [P, 2, P])
        a_in = sb("a_in", [H, P])
        a_t = sb("a_t", [P, H])
        half = sb("half", [P, TT])
        eps = sb("eps", [P, TT])
        wstat = sb("wstat", [P, 8])

        e_sb = sb("e_sb", [P, 2, SEG])
        d_sb = sb("d_sb", [P, 2, SEG])
        a_sb = sb("a_sb", [P, 2, SEG])
        b_sb = sb("b_sb", [P, 2, SEG])
        hs = sb("hs", [P, 2, HG, SEG])
        carry = sb("carry", [P, H])
        bsp = sb("bsp", [P, 2, 3, SEG], BF16)
        dsp = sb("dsp", [K3, 2, SEG], BF16)
        c_seg = sb("c_seg", [P, 2, SEG])
        c_cur = sb("c_cur", [P, SEG])
        ym = sb("ym", [P, 512])
        yh = sb("yh", [P, 512 // BLK, BLK // 2])
        SLOTS = SEGS * GROUPS + 1
        y_tok = sb("y_tok", [P, TILES, SLOTS * HG])

        xp = sb("xp", [P, 2, TT, DM])
        stat = sb("stat", [P, STEPS, TT, 6])
        pause = sb("pause", [P, 2])
        mv = sb("mv", [P, STEPS, TT, 2])
        vpe = sb("vpe", [P, STEPS, TT])
        rstd = sb("rstd", [P, STEPS, TT])
        xn = sb("xn", [P, TT, DM])
        xnt = sb("xnt", [P, 2, 3 * SEG])
        res_b = sb("res_b", [P, STEP])
        res_d = sb("res_d", [K3, STEP])
        hi_d = sb("hi_d", [K3, STEP], BF16)
        mid_d = sb("mid_d", [K3, STEP], BF16)

        xe = sb("xe", [P, 2, TT, DM])
        xs = sb("xs", [P, 2, STEP])
        ys = sb("ys", [P, TT, H, DM // H])
        rows = ys[0:3, :, :, :].rearrange("p t h e -> p t (h e)")
        sg = sb("sg", [P, 2, 512])
        yfull = sb("yfull", [P, 2, STEP])
        tt_f = sb("tt_f", [P, 512])
        prod = sb("prod", [P, 512])

        ring_free = (SEGS - 3) % 3 * SEG
        gate_l = [xnt[:, T // 2, ring_free + 512 * (T % 2):ring_free + 512 * (T % 2) + 512] for T in range(STEPS)]
        silu_l = ([c_seg[:, 0, 512 * T:512 * T + 512] for T in range(2)]
                  + [xp[:, T, :, :].rearrange("p t d -> p (t d)") for T in range(2)])

        def quarters(buf):
            flat = buf[:, :, :].rearrange("p a n -> p (a n)")
            return [flat[:, 512 * T:512 * T + 512] for T in range(STEPS)]

        def ring(s, k, i, more=0):
            if isinstance(k, int):
                first = STEP * (4 * s + 2 * k + i + more) % (3 * SEG)
                return slice(first, first + STEP)
            return bass.ds(STEP * (4 * s + i + more + 2 * k), STEP)

        def p_front(s, g):
            return s + 1 < SEGS and not (s + 2 == SEGS and isinstance(g, int) and g == GROUPS - 1)

        def cols_of(k, i):
            return bass.ds(STEP * (2 * k + i), STEP)

        def pairs(eng, s, groups):
            if s < 2:
                with eng.Fori(0, 2) as k:
                    groups(k)
            else:
                for k in range(2):
                    groups(k)

        x_first = (xp[:, 0], xp[:, 1], xe[:, 0], xe[:, 1])
        xn_first = [q.rearrange("p (t d) -> p t d", t=TT) for q in quarters(e_sb)]
        xt_first = (m0[:, :], y_ps[:, :], m0[:, :], y_ps[:, :])
        proj_first = (m12[:, :, :], z_ps[:, 1, :].rearrange("p (a n) -> p a n", a=2)) * 2

        y_last = (y_ps[:, :], z_ps[:, 0, 0:512], z_ps[:, 1, 0:512], z_ps[:, 1, 512:1024])
        m_last = (m12[:, 0, :], z_ps[:, 0, 512:1024], m12[:, 1, :], m0[:, :])
        ym_last, ys_last, yfull_last, prod_last = quarters(e_sb), quarters(d_sb), quarters(a_sb), quarters(b_sb)
        xe_tail = hs[:, 0, 0, :].rearrange("p (a t d) -> p a t d", a=2, t=TT)

        w_in = {name: sem(name + "_in") for name in ("consts", "Wx", "Wf", "A", "Dp", "bg", "bf", "Wg", "Wo")}
        setup_v, setup_p, setup_pe, setup_a = sem("setup_v"), sem("setup_p"), sem("setup_pe"), sem("setup_a")
        z_ready, exp_done, ln_done = sem("z_ready"), sem("exp_done"), sem("ln_done")
        d_ready, a_ready, b_ready, h_ready = sem("d_ready"), sem("a_ready"), sem("b_ready"), sem("h_ready")
        carry_done, y_ready, y_masked, y_done = sem("carry_done"), sem("y_ready"), sem("y_masked"), sem("y_done")
        c_cur_ready = sem("c_cur_ready")
        y_halved = sem("y_halved")
        rows_copied, rows_left = sem("rows_copied"), sem("rows_left")
        x_in = [sem(f"x_in{i}") for i in range(4)]
        stat_done, aggr_done, vpe_done, rstd_done = sem("stat_done"), sem("aggr_done"), sem("vpe_done"), sem("rstd_done")
        xn_done, xt_ready, xnt_done, proj_ready = sem("xn_done"), sem("xt_ready"), sem("xnt_done"), sem("proj_ready")
        hi_done, res_done, mid_done, split_done = sem("hi_done"), sem("res_done"), sem("mid_done"), sem("split_done")
        xe_in = [sem("xe_in0"), sem("xe_in1")]
        xs_ready, n_ready, nexp_done, nln_done = sem("xs_ready"), sem("n_ready"), sem("nexp_done"), sem("nln_done")
        sp_done, sg_done, silu_done = sem("sp_done"), sem("sg_done"), sem("silu_done")
        ys_ready, mix_ready = sem("ys_ready"), sem("mix_ready")
        yfull_done, s_ready, prod_done = sem("yfull_done"), sem("s_ready"), sem("prod_done")
        l_n_ready, l_nexp_done, l_nln_done = sem("l_n_ready"), sem("l_nexp_done"), sem("l_nln_done")
        l_sp_done, l_sg_done, l_silu_done, l_gate_done = (sem("l_sp_done"), sem("l_sg_done"), sem("l_silu_done"),
                                                          sem("l_gate_done"))
        xe_tail_in, last_out_done, tail_stored = sem("xe_tail_in"), sem("last_out_done"), sem("tail_stored")
        out_done = sem("out_done")
        stored = [sem("stored0"), sem("stored1")]

        x_rows = x.rearrange("b (t p) d -> p (b t) d", p=P)
        out_rows = out.rearrange("b (t p) d -> p (b t) d", p=P)

        marks = {}
        block = ctx.enter_context(nc.Block())

        @block.sync
        def _(sp):
            def load_p(T, i, wait):
                if wait:
                    sp.wait_ge(xn_done, T - 1)
                sp.dma_start(xp[:, i, :, :], x_rows[:, bass.ds(TT * T, TT), :]).then_inc(x_in[i], 16)

            def load_e(T, i, pair, wait):
                if wait:
                    sp.wait_ge(stored[i], 16 * pair)
                sp.dma_start(xe[:, i, :, :], x_rows[:, bass.ds(TT * T, TT), :]).then_inc(xe_in[i], 16)

            def store_e(T, i):
                sp.wait_ge(out_done, T + 1)
                sp.dma_start(out_rows[:, bass.ds(TT * T, TT), :], xe[:, i, :, :]).then_inc(stored[i], 16)

            load_p(0, 0, False)
            sp.dma_start(cst[:, :], consts).then_inc(w_in["consts"], 16)
            load_p(1, 1, False)
            sp.dma_start(wx[:, :, :], Wx.rearrange("(c k) n -> k c n", k=P)).then_inc(w_in["Wx"], 16)
            for T in (2, 3):
                sp.dma_start(xe[:, T % 2, :, :], x_rows[:, TT * T:TT * T + TT, :]).then_inc(x_in[T % 2 + 2], 16)
            for T in (4, 5, 6):
                load_p(T, T % 2, True)
            load_e(0, 0, 0, False)
            load_e(1, 1, 0, False)
            with sp.Fori(0, 2) as kk:
                for i in range(2):
                    load_p(2 * kk + i + 7, 1 - i, True)
            with sp.Fori(2, 4) as kk:
                for i in range(2):
                    load_p(2 * kk + i + 7, 1 - i, True)
                    store_e(2 * kk + i - 4, i)
                    load_e(2 * kk + i - 2, i, kk - 1, True)
            load_p(NSTEPS - 1, 1, True)
            with sp.Fori(4, 8) as kk:
                for i in range(2):
                    store_e(2 * kk + i - 4, i)
                    load_e(2 * kk + i - 2, i, kk - 1, True)
            sp.wait_ge(y_masked, PARTS * (NSTEPS - 1) + PARTS + 1)
            sp.dma_start(xe_tail, x_rows[:, TT * (NSTEPS - 2):TT * NSTEPS, :].rearrange("p (a t) d -> p a t d", a=2)
                         ).then_inc(xe_tail_in, 16)
            for T in (NSTEPS - 4, NSTEPS - 3):
                store_e(T, T % 2)
            sp.wait_ge(out_done, NSTEPS - 1)
            sp.dma_start(out_rows[:, TT * (NSTEPS - 2):TT * (NSTEPS - 1), :], xe_tail[:, 0]).then_inc(tail_stored, 16)
            sp.wait_ge(last_out_done, 1)
            sp.dma_start(out_rows[:, TT * (NSTEPS - 1):TT * NSTEPS, :], xe_tail[:, 1]).then_inc(tail_stored, 16)
            for i in range(2):
                sp.wait_ge(stored[i], 16 * (NSTEPS // 2 - 1))
            sp.wait_ge(tail_stored, 2 * 16)

        @block.gpsimd
        def _(pool):
            def p_rstd(s, k, i, q=0):
                T = 4 * s + 2 * k + i
                pool.wait_ge(aggr_done, 2 * T + 2)
                nc.gpsimd.tensor_tensor(vpe[:, q, :], mv[:, q, :, 1], eps[:, :], ALU.add).then_inc(vpe_done, 1)
                pool.wait_ge(vpe_done, T + 1)
                nc.gpsimd.tensor_tensor(rstd[:, q, :], vpe[:, q, :], half[:, :], ALU.pow).then_inc(rstd_done, 1)

            def e_xs(s, k, i, used=True):
                if used:
                    pool.wait_ge(n_ready, 2 * (4 * s + 2 * k + i))
                nc.gpsimd.tensor_copy(xs[:, :, :], xnt[:, :, ring(s, k, i)]).then_inc(xs_ready, 1)

            def e_out(s, k, i, product=prod[:, :], res=None):
                T = 4 * s + 2 * k + i
                if res is None:
                    res = xe[:, i, :, :]
                    pool.wait_ge(xe_in[i], 16 * (2 * s + k) + 16)
                else:
                    pool.wait_ge(xe_tail_in, 16)
                pool.wait_ge(prod_done, T + 2)
                nc.gpsimd.tensor_tensor(res, res, product.rearrange("p (a d) -> p a d", a=TT), ALU.subtract
                                        ).then_inc(out_done, 1)

            nc.gpsimd.memset(half[:, :], -0.5)
            nc.gpsimd.memset(eps[:, :], LN_EPS).then_inc(setup_p, 1)
            pool.wait_ge(setup_p, 1)
            for T in range(STEPS):
                p_rstd(0, T // 2, T % 2, T)
            nc.gpsimd.memset(ones_bf[:, :], 1.0).then_inc(setup_p, 1)
            nc.gpsimd.memset(c_cur[:, :], 0.0)
            nc.gpsimd.memset(hs[:, 1, :, :], 0.0).then_inc(h_ready, 1)
            pool.wait_ge(xnt_done, 1)
            e_xs(0, 0, 0, False)
            p_rstd(0, 2, 0)

            def last_states(G, g, i):
                pool.wait_ge(h_ready, HG * G + HG + 1)
                nc.gpsimd.tensor_copy(carry[:, bass.ds(HG * g, HG)], hs[:, i, :, SEG - 1]).then_inc(carry_done, 1)

            for s in range(SEGS):

                def groups(k):
                    for i in range(2):
                        g = 2 * k + i
                        G = 4 * s + g
                        has_e = s > 0
                        for j in range(HG):
                            U = HG * G + j
                            pool.wait_ge(d_ready, U + 3)
                            nc.gpsimd.tensor_tensor(b_sb[:, j % 2, :], d_sb[:, j % 2, :], d_sb[:, j % 2, :],
                                                    ALU.mult).then_inc(b_ready, 1)
                            if j % 2 == 1:
                                pool.wait_ge(y_masked, PARTS * G + j // 2 + 2)
                                blocks = ym[:, :].rearrange("p (a l) -> p a l", l=BLK)
                                nc.gpsimd.tensor_tensor(yh[:, :, :], blocks[:, :, 0:BLK // 2], blocks[:, :, BLK // 2:BLK],
                                                        ALU.add).then_inc(y_halved, 1)
                            if j % 2 == 0 and (j > 0 if i == 0 else j == 0):
                                part = (j // 2 - 1) % PARTS
                                piece = slice(STEP * part, STEP * part + STEP)
                                nc.gpsimd.tensor_scalar(c_cur[:, piece], c_seg[:, s % 2, piece], 1.0, 0.0, ALU.mult,
                                                        ALU.add).then_inc(c_cur_ready, 1)
                            if j == 3 and s == 1:
                                e_xs(s - 1, k, i + 1)
                            if j == 4 and p_front(s, g):
                                p_rstd(s + 1, k, i + 1)
                            if j == 7 and has_e:
                                e_out(s - 1, k, i)
                            if j == 1 and i == 1 and s % 2 == 0:
                                last_states(G - 1, g - 1, 0)
                    if s % 2 == 0:
                        last_states(G, g, 1)
                pairs(pool, s, groups)
            for T in range(STEPS - 1):
                e_out(SEGS - 1, T // 2, T % 2, prod_last[T], xe_tail[:, 0] if T >= 2 else None)

        @block.scalar
        def _(act):
            def p_xnt(s, k, i, xt=m0[:, :]):
                T = 4 * s + 2 * k + i
                act.wait_ge(xt_ready, T + 1)
                nc.scalar.activation(xnt[:, :, ring(s, k, i)],
                                     xt.rearrange("p (a t) -> p a t", a=2), ACT.Copy).then_inc(xnt_done, 1)

            def p_hi_d(s, k, i, proj=m12):
                act.wait_ge(proj_ready, 2 * (4 * s + 2 * k + i) + 1)
                nc.scalar.activation(hi_d[:, :], proj[0:K3, 0, 0:STEP], ACT.Copy)

            def p_hi(s, k, i, proj=m12):
                cols = cols_of(k, i)
                act.wait_ge(proj_ready, 2 * (4 * s + 2 * k + i) + 2)
                nc.scalar.activation(bsp[:, s % 2, 0, cols], proj[:, 1, 0:STEP], ACT.Copy)
                nc.scalar.activation(c_seg[:, s % 2, cols], proj[:, 1, STEP:2 * STEP], ACT.Copy).then_inc(hi_done, 1)

            def p_mid(s, k, i):
                T = 4 * s + 2 * k + i
                act.wait_ge(res_done, T + 2)
                nc.scalar.activation(bsp[:, s % 2, 1, cols_of(k, i)], res_b[:, :], ACT.Copy)
                nc.scalar.activation(mid_d[:, :], res_d[:, :], ACT.Copy).then_inc(mid_done, 1)

            def e_ln(s, k, i, q):
                n = 2 * (4 * s + 2 * k + i) + q + 1
                act.wait_ge(n_ready, n)
                nc.scalar.activation(sg[:, q, :], m12[:, q, :], ACT.Exp).then_inc(nexp_done, 1)
                if q:
                    e_sg(s, k, i, 0)
                act.wait_ge(nexp_done, n)
                nc.scalar.activation(sg[:, q, :], sg[:, q, :], ACT.Ln, bias=1.0).then_inc(nln_done, 1)

            def e_sg(s, k, i, q):
                act.wait_ge(sp_done, 2 * (4 * s + 2 * k + i) + q + 1)
                nc.scalar.activation(sg[:, q, :], sg[:, q, :], ACT.Exp, scale=-1.0).then_inc(sg_done, 1)

            def l_ln(T, q):
                act.wait_ge(l_n_ready, 2 * T + q + 1)
                if q:
                    act.wait_ge(yfull_done, 4 * (SEGS - 2) + T + 1)
                nc.scalar.activation(sg[:, q, :], m12[:, q, :], ACT.Exp).then_inc(l_nexp_done, 1)
                act.wait_ge(l_nexp_done, 2 * T + q + 1)
                nc.scalar.activation(sg[:, q, :], sg[:, q, :], ACT.Ln, bias=1.0).then_inc(l_nln_done, 1)

            def l_sg(T):
                act.wait_ge(l_sp_done, 2 * T + 1)
                nc.scalar.activation(sg[:, 0, :], sg[:, 0, :], ACT.Exp, scale=-1.0).then_inc(l_sg_done, 1)

            nc.scalar.preload_act_table_set("natural_log_exp_and_others")
            act.dma_start(xs_w := yfull[:, :, :], Wf.rearrange("(c o) i -> o c i", o=P)).then_inc(w_in["Wf"], 16)
            act.dma_start(a_in[:, :], A).then_inc(w_in["A"], 16)
            act.dma_start(dp_in[:, :], Dp.rearrange("(h o) -> h o", o=1)).then_inc(w_in["Dp"], 16)
            act.dma_start(rows[:, 0, :], bg[None, :].to_broadcast([3, DM])).then_inc(w_in["bg"], 16)
            act.dma_start(rows[:, 1, :], bf[None, :].to_broadcast([3, DM])).then_inc(w_in["bf"], 16)
            act.dma_start(wgn[:, :, :], Wg.rearrange("(c k) n -> k c n", k=P)).then_inc(w_in["Wg"], 16)
            act.dma_start(wo[:, :, :], Wo.rearrange("(c k) n -> k c n", k=P)).then_inc(w_in["Wo"], 16)
            act.wait_ge(w_in["consts"], 16)
            nc.scalar.activation(ident_bf[:, :], ident, ACT.Copy).then_inc(setup_a, 1)
            act.wait_ge(w_in["Wf"], 16)
            nc.scalar.activation(prod[:, :], xs_w.rearrange("p a b -> p (a b)"), ACT.Abs).then_inc(setup_a, 1)

            def selectors(c):
                heads = slice(H // 2 * c, H // 2 * c + H // 2)
                nc.scalar.activation(sel[:, heads, :], cst[:, C_EYE + H // 2 * c:C_EYE + H // 2 * c + H // 2, None]
                                     .to_broadcast([P, H // 2, P]), ACT.Copy)

            p_xnt(0, 0, 0, xt_first[0])
            selectors(0)
            p_xnt(0, 0, 1, xt_first[1])
            selectors(1)
            for T in range(STEPS):
                p_hi_d(0, T // 2, T % 2, proj_first[T])
                p_hi(0, T // 2, T % 2, proj_first[T])
                if T + 2 < STEPS:
                    p_xnt(0, (T + 2) // 2, T % 2, xt_first[T + 2])
                p_mid(0, T // 2, T % 2)
                if T == 0:
                    act.wait_ge(setup_pe, 1)
                    nc.scalar.activation(a_t[:, :], z_ps[:, 0, 0:H], ACT.Copy).then_inc(setup_a, 1)
                    nc.scalar.activation(dp[:, :], z_ps[:, 0, H:H + 2], ACT.Copy).then_inc(setup_a, 1)
                if T == 1:
                    act.wait_ge(w_in["bg"], 16)
                    act.wait_ge(w_in["bf"], 16)
                    nc.scalar.activation(rows[:, :, :], rows[:, :, :], ACT.Copy, scale=-1.0).then_inc(setup_a, 1)
                if T == 2:
                    act.wait_ge(setup_a, 5)
                    nc.scalar.activation(rows_hi[:, :, :], rows[:, :, :], ACT.Copy).then_inc(rows_copied, 1)
            act.wait_ge(rows_left, 1)
            nc.scalar.activation(rows_hi[:, :, :], rows[:, :, :], ACT.Copy).then_inc(rows_copied, 1)
            act.wait_ge(setup_pe, 3)
            nc.scalar.activation(wfn[:, :, :], m0[:, :].rearrange("p (a o) -> p a o", a=2),
                                 ACT.Copy, scale=-1.0).then_inc(setup_a, 1)
            act.wait_ge(w_in["Wg"], 16)
            nc.scalar.activation(wgn[:, :, :], wgn[:, :, :], ACT.Copy, scale=-1.0).then_inc(setup_a, 1)

            def unit_a(G, g, j):
                act.wait_ge(d_ready, HG * G + j + 3)
                nc.scalar.activation(a_sb[:, j % 2, :], d_sb[:, j % 2, :], ACT.Exp,
                                     scale=a_t[:, bass.ds(HG * g + j, 1)]).then_inc(a_ready, 1)

            for s in range(SEGS):

                def groups(k):
                    for i in range(2):
                        g = 2 * k + i
                        G = 4 * s + g
                        has_p, has_e = s + 1 < SEGS, s > 0
                        for j in range(HG):
                            U = HG * G + j
                            act.wait_ge(z_ready, U + 1)
                            nc.scalar.activation(e_sb[:, j % 2, :], z_ps[:, j % 2, :], ACT.Exp).then_inc(exp_done, 1)
                            if j == 3 and has_e:
                                e_sg(s - 1, k, i, 1)
                            act.wait_ge(exp_done, U + 1)
                            nc.scalar.activation(e_sb[:, j % 2, :], e_sb[:, j % 2, :], ACT.Ln, bias=1.0).then_inc(ln_done, 1)
                            if j > 0:
                                unit_a(G, g, j - 1)
                            elif i > 0:
                                unit_a(G - 1, g - 1, HG - 1)
                            if j == 0 and has_e:
                                e_ln(s - 1, k, i, 0)
                            if j == 1 and has_e:
                                e_ln(s - 1, k, i, 1)
                            if j == 2 and has_p:
                                p_xnt(s + 1, k, i)
                            if j == 4 and has_p:
                                p_hi_d(s + 1, k, i)
                                p_hi(s + 1, k, i)
                            if j == 4 and not has_p:
                                l_ln(g, 0)
                            if j == 5 and has_p:
                                p_mid(s + 1, k, i)
                            if j == 5 and not has_p:
                                l_sg(g)
                            if j == 6 and not has_p:
                                l_ln(g, 1)
                    unit_a(G, g, HG - 1)
                pairs(act, s, groups)
            for T in range(STEPS):
                act.wait_ge(l_sp_done, 2 * T + 2)
                nc.scalar.activation(gate_l[T], gate_l[T], ACT.Exp, scale=-1.0).then_inc(l_gate_done, 1)

        @block.vector
        def _(dve):
            vs = [0]

            def own(ins):
                vs[0] += 1
                ins.then_inc(setup_v, 1)
                dve.wait_ge(setup_v, vs[0])

            def p_stats(s, k, i, src=None, q=0):
                T = 4 * s + 2 * k + i
                if s == 0 and T < STEPS:
                    dve.wait_ge(x_in[T], 16)
                else:
                    dve.wait_ge(x_in[i % 2], 16 * (2 * s + k + i // 2))
                src = xp[:, i % 2] if src is None else src
                for t in range(TT):
                    nc.vector.bn_stats(stat[:, q, t, :], src[:, t, :]).then_inc(stat_done, 1)
                dve.wait_ge(stat_done, TT * T + TT)
                nc.vector.memset(pause[:, :], 0.0)
                for t in range(TT):
                    nc.vector.bn_aggr(mv[:, q, t, :], stat[:, q, t, :]).then_inc(aggr_done, 1)

            def p_norm(s, k, i, src=None, dst=xn, q=0):
                src = xp[:, i % 2] if src is None else src
                dve.wait_ge(rstd_done, 4 * s + 2 * k + i + 1)
                for t in range(TT):
                    ins = nc.vector.tensor_scalar(dst[:, t, :], src[:, t, :], mv[:, q, t, 0:1], rstd[:, q, t:t + 1],
                                                  ALU.subtract, ALU.mult)
                ins.then_inc(xn_done, 1)

            def p_res(s, k, i, proj=m12):
                dve.wait_ge(hi_done, 4 * s + 2 * k + i + 1)
                nc.vector.tensor_tensor(res_b[:, :], proj[:, 1, 0:STEP],
                                        bsp[:, s % 2, 0, cols_of(k, i)], ALU.subtract)
                nc.vector.scalar_tensor_tensor(res_d[:, :], hi_d[:, :], cst[0:K3, C_KEEP:C_KEEP + 1],
                                               proj[0:K3, 0, 0:STEP], ALU.mult, ALU.add).then_inc(res_done, 1)

            def p_low(s, k, i):
                cols = cols_of(k, i)
                dve.wait_ge(mid_done, 4 * s + 2 * k + i + 1)
                nc.vector.tensor_tensor(bsp[:, s % 2, 2, cols], res_b[:, :], bsp[:, s % 2, 1, cols], ALU.subtract)
                nc.vector.scalar_tensor_tensor(dsp[:, s % 2, cols], mid_d[:, :], cst[0:K3, C_KEEP + 1:C_KEEP + 2],
                                               res_d[:, :], ALU.mult, ALU.add).then_inc(split_done, 1)

            def e_sp(s, k, i, q):
                dve.wait_ge(nln_done, 2 * (4 * s + 2 * k + i) + q + 1)
                nc.vector.scalar_tensor_tensor(sg[:, q, :], sg[:, q, :], SP_CLAMP, m12[:, q, :], ALU.min, ALU.max
                                               ).then_inc(sp_done, 1)

            def e_silu(s, k, i):
                dve.wait_ge(sg_done, 2 * (4 * s + 2 * k + i) + 1)
                nc.vector.tensor_tensor(tt_f[:, :], m12[:, 0, :], sg[:, 0, :], ALU.mult).then_inc(silu_done, 1)

            def l_sp(T, q):
                dst = gate_l[T] if q else sg[:, 0, :]
                dve.wait_ge(l_nln_done, 2 * T + q + 1)
                nc.vector.scalar_tensor_tensor(dst, sg[:, q, :], SP_CLAMP, m12[:, q, :], ALU.min, ALU.max).then_inc(l_sp_done, 1)

            def l_silu(T):
                dve.wait_ge(l_sg_done, T + 1)
                nc.vector.tensor_tensor(silu_l[T], m12[:, 0, :], sg[:, 0, :], ALU.mult).then_inc(l_silu_done, 1)

            def e_ys(s, k, i, dst=ys[:, :, :, :]):
                if s == SEGS - 1:
                    dve.wait_ge(y_done, PARTS * SEGS * GROUPS + 2 * k + i + 2)
                nc.vector.tensor_copy(dst, y_tok[:, bass.ds(TT * (2 * k + i), TT), HG + H * s:HG + H * s + H, None]
                                      .to_broadcast([P, TT, H, DM // H])).then_inc(ys_ready, 1)

            def e_yfull(s, k, i, m=m0[:, :], gate=None, dst=yfull[:, :, :]):
                T = 4 * s + 2 * k + i
                dve.wait_ge(mix_ready, T + 1)
                if gate is None:
                    gate = sg[:, 1, :]
                    dve.wait_ge(sg_done, 2 * T + 2)
                else:
                    dve.wait_ge(l_gate_done, T % STEPS + 1)
                nc.vector.tensor_tensor(dst, m.rearrange("p (a t) -> p a t", a=2), gate.rearrange("p (a t) -> p a t", a=2),
                                        ALU.mult).then_inc(yfull_done, 1)

            def e_prod(s, k, i, m=m0[:, :], silu=None, dst=prod[:, :]):
                T = 4 * s + 2 * k + i
                dve.wait_ge(s_ready, T + 1)
                if silu is None:
                    silu = tt_f[:, :]
                    dve.wait_ge(silu_done, T + 1)
                nc.vector.tensor_tensor(dst, m, silu, ALU.mult).then_inc(prod_done, 1)

            def y_mask(G, p, bank=y_ps[:, :], dst=ym[:, :]):
                dve.wait_ge(y_ready, PARTS * G + p + 1)
                dve.wait_ge(y_done, PARTS * G + p + 1)
                nc.vector.tensor_tensor(dst.rearrange("p (a l) -> p a l", l=BLK),
                                        bank.rearrange("p (a l) -> p a l", l=BLK),
                                        mask[:, None, :].to_broadcast([P, 512 // BLK, BLK]), ALU.mult).then_inc(y_masked, 1)

            def y_sum(G, p, src=None):
                if src is None:
                    src = yh[:, :, :].rearrange("p (t h) l -> p t h l", t=2)
                    dve.wait_ge(y_halved, PARTS * G + p + 1)
                else:
                    src = src.rearrange("p (t h l) -> p t h l", t=2, l=BLK)
                    dve.wait_ge(y_masked, PARTS * G + p + 2)
                nc.vector.tensor_reduce(y_tok[:, 2 * p:2 * p + 2, bass.ds(HG * G, HG)], src, AX_X, ALU.add
                                        ).then_inc(y_done, 1)

            def unit_d(G, j):
                dve.wait_ge(ln_done, HG * G + j + 1)
                nc.vector.scalar_tensor_tensor(d_sb[:, j % 2, :], e_sb[:, j % 2, :], SP_CLAMP, z_ps[:, j % 2, :],
                                               ALU.min, ALU.max).then_inc(d_ready, 1)

            def unit_scan(s, G, g, j, i):
                U = HG * G + j
                dve.wait_ge(a_ready, U + 1)
                dve.wait_ge(b_ready, U + 1)
                start = carry[:, bass.ds(HG * g + j, 1)] if s % 2 else 0.0
                nc.vector.tensor_tensor_scan(hs[:, i, j, :], a_sb[:, j % 2, :], b_sb[:, j % 2, :], start,
                                             ALU.mult, ALU.add).then_inc(h_ready, 1)

            def stats0(T):
                p_stats(0, T // 2, T % 2, x_first[T], T)

            def norm0(T):
                p_norm(0, T // 2, T % 2, x_first[T], xn_first[T], T)

            def res0(T):
                if T > 0:
                    dve.wait_ge(split_done, T)
                p_res(0, T // 2, T % 2, proj_first[T])

            def low0(T):
                p_low(0, T // 2, T % 2)

            dve.sem_inc(res_done, 1)
            dve.sem_inc(d_ready, 2)
            dve.sem_inc(y_masked, 1)
            dve.sem_inc(y_done, 1)
            dve.sem_inc(prod_done, 1)

            nc.vector.memset(ones[:, :], 1.0)
            stats0(0)
            norm0(0)
            stats0(1)
            dve.wait_ge(w_in["Wx"], 16)
            for r in range(3):
                ins = nc.vector.tensor_copy(wdb[:, :, r, :], wx[:, :, 2 * N:2 * N + H])
            own(ins)
            marks["wdb"] = vs[0]
            norm0(1)
            stats0(2)
            stats0(3)
            norm0(2)
            norm0(3)
            wf = yfull[:, :, :].rearrange("p a b -> p (a b)")
            dve.wait_ge(setup_a, 2)
            own(nc.vector.reduce_sum(wstat[:, 0:1], prod[:, :], AX_X))
            marks["wsum"] = vs[0]
            res0(0)
            dve.wait_ge(setup_pe, 2)
            own(nc.vector.tensor_scalar(wstat[:, 1:2], z_ps[:, 0, 512:513], 1.0 / (DM * DM), None, ALU.mult))
            low0(0)
            own(nc.vector.tensor_scalar(wstat[:, 2:3], wstat[:, 1:2], W_EPS, None, ALU.add))
            nc.vector.tensor_scalar(wstat[:, 3:4], wstat[:, 2:3], 0.5, None, ALU.mult)
            own(nc.vector.tensor_scalar(wstat[:, 4:5], wstat[:, 2:3], -0.5, None, ALU.mult))
            nc.vector.tensor_scalar(tt_f[:, :], wf, wstat[:, 3:4], None, ALU.is_gt)
            res0(1)
            own(nc.vector.tensor_scalar(prod[:, :], wf, wstat[:, 4:5], None, ALU.is_lt))
            low0(1)
            own(nc.vector.tensor_tensor(tt_f[:, :], tt_f[:, :], prod[:, :], ALU.subtract))
            res0(2)
            own(nc.vector.scalar_tensor_tensor(prod[:, :], tt_f[:, :], wstat[:, 1:2], wf, ALU.mult, ALU.subtract))
            low0(2)
            own(nc.vector.tensor_tensor(tt_f[:, :], wf, prod[:, :], ALU.add))
            marks["wf"] = vs[0]

            def rows_rest(part, dst):
                dve.wait_ge(rows_copied, part + 1)
                keep = cst[0:3, C_KEEP1 + part:C_KEEP1 + part + 1]
                nc.vector.scalar_tensor_tensor(dst[:, :, :], rows_hi[:, :, :], keep, rows[:, :, :], ALU.mult, ALU.add
                                               ).then_inc(rows_left, 1)

            res0(3)
            rows_rest(0, rows)
            low0(3)
            dve.wait_ge(setup_a, 4)
            for c in range(2):
                nc.vector.tensor_scalar(dp_diag[:, c, :], ident, dp[:, c:c + 1], None, ALU.mult)
            rows_rest(1, rows_bf)
            p_stats(0, 2, 0)
            p_norm(0, 2, 0)

            for s in range(SEGS):
                if s % 2:
                    dve.wait_ge(carry_done, 4 * (s // 2) + 4)

                def groups(k):
                    for i in range(2):
                        g = 2 * k + i
                        G = 4 * s + g
                        has_p, has_e = s + 1 < SEGS, s > 0
                        for j in range(HG):
                            unit_d(G, j)
                            if j % 2 == 1:
                                y_mask(G, j // 2)
                            if j == 3 and has_e:
                                e_ys(s - 1, k, i)
                            if j == 5 and has_e:
                                e_yfull(s - 1, k, i)
                            if j == 7 and has_e and not (s == SEGS - 1 and g == GROUPS - 1):
                                e_prod(s - 1, k, i)
                            if j > 0:
                                unit_scan(s, G, g, j - 1, i)
                            elif i > 0:
                                unit_scan(s, G - 1, g - 1, HG - 1, i - 1)
                            if j > 0 and j % 2 == 0:
                                y_sum(G, j // 2 - 1)
                            if j == 0 and i > 0:
                                y_sum(G - 1, PARTS - 1)
                            if j == 0 and has_e:
                                e_sp(s - 1, k, i, 0)
                            if j == 1 and has_e:
                                e_silu(s - 1, k, i)
                                e_sp(s - 1, k, i, 1)
                            if j == 2 and p_front(s, g):
                                p_stats(s + 1, k, i + 1)
                            if j == 4 and has_p:
                                p_res(s + 1, k, i)
                            if j == 4 and not has_p:
                                l_sp(g, 0)
                            if j == 5 and has_p:
                                p_low(s + 1, k, i)
                            if j == 5 and not has_p:
                                l_silu(g)
                            if j == 6 and not has_p:
                                l_sp(g, 1)
                            if j == 6 and p_front(s, g):
                                p_norm(s + 1, k, i + 1)
                    unit_scan(s, G, g, HG - 1, 1)
                    if s == SEGS - 1 and g == GROUPS - 1:
                        e_prod(s - 1, k, i)
                    y_sum(G, PARTS - 1)
                pairs(dve, s, groups)
            for T in range(STEPS + 2):
                if T < STEPS:
                    y_mask(SEGS * GROUPS, T, y_last[T], ym_last[T])
                    y_sum(SEGS * GROUPS, T, ym_last[T])
                    e_ys(SEGS - 1, T // 2, T % 2, ys_last[T].rearrange("p (t h e) -> p t h e", t=TT, h=H))
                if 1 <= T <= STEPS:
                    e_yfull(SEGS - 1, (T - 1) // 2, (T - 1) % 2, m_last[T - 1], gate_l[T - 1],
                            yfull_last[T - 1].rearrange("p (a n) -> p a n", a=2))
                if T >= 2:
                    e_prod(SEGS - 1, (T - 2) // 2, T % 2, m_last[T - 2], silu_l[T - 2],
                           prod_last[T - 2])
            dve.wait_ge(xe_tail_in, 16)
            dve.wait_ge(prod_done, NSTEPS + 1)
            nc.vector.tensor_tensor(xe_tail[:, 1], xe_tail[:, 1], prod_last[STEPS - 1].rearrange("p (a d) -> p a d", a=TT),
                                    ALU.subtract).then_inc(last_out_done, 1)

        @block.tensor
        def _(pe):
            def unit_z(s, G, g, j, first):
                pe.wait_ge(d_ready, HG * G + j + 1)
                for halves in ((0,), (1,)) if first else ((0, 1),):
                    if first:
                        pe.wait_ge(split_done, 4 * s + 2 * halves[0] + 2)
                    for r in range(3):
                        for c in halves:
                            nc.tensor.matmul(z_ps[:, j % 2, 512 * c:512 * c + 512], ident_bf[:, :],
                                             bsp[:, s % 2, r, 512 * c:512 * c + 512], start=(r == 0), stop=False)
                    for c in halves:
                        ins = nc.tensor.matmul(z_ps[:, j % 2, 512 * c:512 * c + 512], sel[0:K3, HG * g + j, :],
                                               dsp[:, s % 2, 512 * c:512 * c + 512], start=False, stop=True)
                ins.then_inc(z_ready, 1)

            def y_part(G, i, p, bank=y_ps):
                Y = PARTS * G + p
                if p == 0:
                    pe.wait_ge(h_ready, HG * G + 1)
                pe.wait_ge(y_masked, Y + 1)
                for q in range(2):
                    for c in range(4):
                        t0 = 256 * p + P * q + BLK * c
                        ins = nc.tensor.matmul(bank[BLK * c:BLK * c + BLK, 256 * q:256 * q + 256],
                                               c_cur[:, t0:t0 + BLK], hs[:, 1 - i, :, t0:t0 + BLK], start=True, stop=True)
                ins.then_inc(y_ready, 1)

            def p_xt(s, k, i, e_before, src=xn, dst=m0):
                T = 4 * s + 2 * k + i
                pe.wait_ge(xn_done, T + 1)
                if e_before is not None:
                    pe.wait_ge(prod_done, e_before + 1)
                for c in range(2):
                    for t in range(TT):
                        ins = nc.tensor.transpose(dst[:, STEP * c + P * t:STEP * c + P * t + P],
                                                  src[:, t, P * c:P * c + P], ident)
                ins.then_inc(xt_ready, 1)

            def p_db(s, k, i, e_now, proj=m12, p_free=None):
                T = 4 * s + 2 * k + i
                cols = ring(s, k, i)
                pe.wait_ge(xnt_done, T + 1)
                pe.wait_ge(res_done, T + 1 if p_free is None else p_free)
                if e_now is not None:
                    pe.wait_ge(silu_done, e_now)
                for c in range(2):
                    ins = nc.tensor.matmul(proj[0:K3, 0, 0:STEP], wdb[:, c, :, :].rearrange("p r h -> p (r h)"),
                                           xnt[:, c, cols], start=(c == 0), stop=(c == 1))
                ins.then_inc(proj_ready, 1)

            def p_bc(s, k, i, e_now, proj=m12):
                cols = ring(s, k, i)
                if e_now is not None:
                    pe.wait_ge(sp_done, 2 * e_now)
                for o in range(2):
                    for c in range(2):
                        ins = nc.tensor.matmul(proj[:, 1, STEP * o:STEP * o + STEP], wx[:, c, P * o:P * o + P],
                                               xnt[:, c, cols], start=(c == 0), stop=(c == 1))
                ins.then_inc(proj_ready, 1)

            def ffn(src, ready):
                for t in range(TT):
                    dst = m12[:, 0, DM * t:DM * t + DM]
                    for c in range(2):
                        nc.tensor.matmul(dst, src[:, c, P * t:P * t + P], wfn[:, c, :], start=(c == 0), stop=False)
                    ins = nc.tensor.matmul(dst, ones_bf[:, 0:P], rows_bf[:, 1, :], start=False, stop=True)
                ins.then_inc(ready, 1)

            def gate(s, k, i, o, ready):
                dst = m12[:, 1, STEP * o:STEP * o + STEP]
                for c in range(2):
                    nc.tensor.matmul(dst, wgn[:, c, P * o:P * o + P], xnt[:, c, ring(s, k, i)],
                                     start=(c == 0), stop=False)
                ins = nc.tensor.matmul(dst, rows_bf[:, 0, P * o:P * o + P], ones_bf[:, :], start=False, stop=True)
                if o == 1:
                    ins.then_inc(ready, 1)

            def e_mix(s, k, i, ys_src=ys, m=m0, x_part=True, y_part=True):
                if y_part:
                    pe.wait_ge(ys_ready, 4 * s + 2 * k + i + 1)
                for c in range(2):
                    dst = m[:, STEP * c:STEP * c + STEP]
                    if x_part:
                        nc.tensor.matmul(dst, dp_diag[:, c, :], xnt[:, c, ring(s, k, i)],
                                         start=(y_part or c == 0), stop=False)
                    for t in range(TT if y_part else 0):
                        ins = nc.tensor.matmul(dst[:, P * t:P * t + P],
                                               ys_src[:, t, H // 2 * c:H // 2 * c + H // 2, :].rearrange("p h e -> p (h e)"),
                                               ident, start=False, stop=(t == TT - 1 and (x_part or c == 1)))
                if y_part:
                    ins.then_inc(mix_ready, 1)

            def e_s(s, k, i, src=yfull, m=m0):
                pe.wait_ge(yfull_done, 4 * s + 2 * k + i + 1)
                for t in range(TT):
                    for c in range(2):
                        ins = nc.tensor.matmul(m[:, DM * t:DM * t + DM], src[:, c, P * t:P * t + P], wo[:, c, :],
                                               start=(c == 0), stop=(c == 1))
                ins.then_inc(s_ready, 1)

            def xt0(T):
                if T >= 2:
                    pe.wait_ge(xnt_done, T - 1)
                p_xt(0, T // 2, T % 2, None, xn_first[T], xt_first[T])

            def proj0(T):
                p_db(0, T // 2, T % 2, None, proj_first[T], T if T >= 2 else 1)
                p_bc(0, T // 2, T % 2, None, proj_first[T])

            pe.wait_ge(w_in["consts"], 16)
            xt0(0)
            pe.wait_ge(w_in["Wx"], 16)
            pe.wait_ge(setup_v, marks["wdb"])
            p_db(0, 0, 0, None, proj_first[0], 1)
            xt0(1)
            p_bc(0, 0, 0, None, proj_first[0])

            pe.wait_ge(w_in["A"], 16)
            pe.wait_ge(w_in["Dp"], 16)
            nc.tensor.transpose(z_ps[:, 0, 0:H], a_in[:, :], ident[0:H, 0:H])
            for c in range(2):
                ins = nc.tensor.matmul(z_ps[:, 0, H + c:H + c + 1], cst[0:H, C_REP + P * c:C_REP + P * c + P],
                                       dp_in[:, :], start=True, stop=True)
            ins.then_inc(setup_pe, 1)
            xt0(2)
            proj0(1)
            pe.wait_ge(setup_v, marks["wsum"])
            nc.tensor.matmul(z_ps[:, 0, 512:513], ones[:, :], wstat[:, 0:1], start=True, stop=True).then_inc(setup_pe, 1)
            xt0(3)
            proj0(2)
            proj0(3)
            pe.wait_ge(setup_v, marks["wf"])
            for c in range(2):
                for o in range(2):
                    ins = nc.tensor.transpose(m0[:, DM * c + P * o:DM * c + P * o + P],
                                              tt_f[:, DM * o + P * c:DM * o + P * c + P], ident)
            ins.then_inc(setup_pe, 1)
            pe.wait_ge(setup_a, 4)
            for s in range(SEGS):

                def groups(k):
                    for i in range(2):
                        g = 2 * k + i
                        G = 4 * s + g
                        has_p, has_e = s + 1 < SEGS, s > 0
                        e_now = 4 * (s - 1) + g if has_e else None
                        p_now = 4 * (s + 1) + g
                        for j in range(HG):
                            unit_z(s, G, g, j, i == 0 and j == 0)
                            if j == 0 and has_e:
                                if has_p:
                                    pe.wait_ge(res_done, p_now + 1)
                                else:
                                    pe.wait_ge(res_done, NSTEPS + 1)
                                    if g > 0:
                                        pe.wait_ge(l_silu_done, g)
                                if s == 1 or (s == 2 and g == 0):
                                    pe.wait_ge(xs_ready, e_now + 1)
                                    ffn(xs, n_ready)
                                else:
                                    ffn(xnt[:, :, ring(s - 1, k, i)], n_ready)
                            if j == 1 and has_p:
                                if s == 0:
                                    pe.wait_ge(setup_a, 6)
                                p_xt(s + 1, k, i, e_now)
                            if j == 1 and has_e:
                                if not has_p and g > 0:
                                    pe.wait_ge(l_sp_done, 2 * g)
                                for o in range(2):
                                    gate(s - 1, k, i, o, n_ready)
                            if i == 1 and j % 2 == 1:
                                pe.wait_ge(c_cur_ready, PARTS * (2 * s + k) + j // 2 + 1)
                            if j % 2 == 1:
                                y_part(G, i, j // 2)
                            if j == 4 and has_p:
                                p_db(s + 1, k, i, e_now + 1 if has_e else None)
                                p_bc(s + 1, k, i, e_now + 1 if has_e else None)
                            if j == 4 and not has_p:
                                pe.wait_ge(silu_done, e_now + 1)
                                ffn(xnt[:, :, ring(s, k, i)], l_n_ready)
                            if j == 5 and has_e:
                                if has_p:
                                    pe.wait_ge(xnt_done, p_now + 1)
                                pe.wait_ge(prod_done, e_now + 1)
                                e_mix(s - 1, k, i)
                            if j == 6 and not has_p:
                                pe.wait_ge(sp_done, 2 * e_now + 2)
                                for o in range(2):
                                    gate(s, k, i, o, l_n_ready)
                            if j == 7 and has_e:
                                e_s(s - 1, k, i)
                if s == 1:
                    pe.wait_ge(rows_left, 2)
                    pe.wait_ge(setup_a, 7)
                    pe.wait_ge(setup_p, 2)
                    pe.wait_ge(w_in["Wo"], 16)
                pairs(pe, s, groups)

            def last_x(T):
                e_mix(SEGS - 1, T // 2, T % 2, None, m_last[T], y_part=False)

            def last_y(T):
                y_part(SEGS * GROUPS, 0, T, y_last[T])

            def last_mix(T):
                e_mix(SEGS - 1, T // 2, T % 2, ys_last[T].rearrange("p (t h e) -> p t h e", t=TT, h=H), m_last[T],
                      x_part=False)

            def last_s(T):
                e_s(SEGS - 1, T // 2, T % 2, yfull_last[T].rearrange("p (a n) -> p a n", a=2), m_last[T])

            pe.wait_ge(l_silu_done, STEPS)
            last_x(0)
            pe.wait_ge(d_ready, SEGS * GROUPS * HG + 1)
            last_x(1)
            pe.wait_ge(l_sp_done, 2 * STEPS)
            last_x(2)
            last_y(0)
            last_y(1)
            last_mix(0)
            last_y(2)
            pe.wait_ge(prod_done, NSTEPS - STEPS + 1)
            last_x(3)
            last_mix(1)
            last_s(0)
            last_y(3)
            last_mix(2)
            last_s(1)
            last_mix(3)
            last_s(2)
            last_s(3)


_INS = ["L0_attn_x", "L0_attn_Wx", "L0_attn_Wg", "L0_attn_bg", "L0_attn_Wo", "L0_attn_A", "L0_attn_Dp",
        "L0_ffn_weight", "L0_ffn_bias"]


def kernel(**inputs):
    import concourse.bacc as _bacc
    from concourse.bass_utils import run_bass_kernel_spmd as _run

    nc = _bacc.Bacc("TRN2", target_bir_lowering=False, num_devices=1)
    arrays, args = {}, []
    for name in _INS:
        a = np.ascontiguousarray(inputs[name])
        arrays[name] = a
        args.append(nc.dram_tensor(name, a.shape, mybir.dt.from_np(a.dtype), kind="ExternalInput").ap())
    heads, dm = arrays["L0_attn_A"].shape[0], arrays["L0_attn_x"].shape[2]
    arrays["shape_constants"] = shape_constants(heads, dm)
    args.append(nc.dram_tensor("shape_constants", (P, C_COLS), F32, kind="ExternalInput").ap())
    args.append(nc.dram_tensor("out", arrays["L0_attn_x"].shape, F32, kind="ExternalOutput").ap())
    program(nc, *args)
    r = _run(nc, [arrays], core_ids=[0])
    return r.results[0]["out"]
```
